# Optimizing a Trainium2 kernel written in Bass

```python
import numpy as np
import jax
import jax.numpy as jnp

def _softmax(x, axis=-1):
    return jax.nn.softmax(x, axis=axis)

def _gelu(x):
    return jax.nn.gelu(x, approximate=True)

def _silu(x):
    return jax.nn.silu(x)

def _sigmoid(x):
    return jax.nn.sigmoid(x)

def _layernorm(x, axis=-1, eps=1e-05):
    m = jnp.mean(x, axis=axis, keepdims=True)
    v = jnp.var(x, axis=axis, keepdims=True)
    return (x - m) / jnp.sqrt(v + eps)

def _scatter_add(tgt, idx, src, axis=0):
    return tgt.at[idx].add(src)

def _segment_sum(src, seg, n):
    return jax.ops.segment_sum(src, seg, n)
kernel_name = 'mk_hybrid_d1_jaxref_r8_423da1'

def setup_inputs(seed: int=0):
    np.random.seed(seed)
    _w = jnp.asarray

    def _L0_attn_a_setup():
        import jax, jax.numpy as jnp
        import numpy as np
        import math
        D_MODEL = 128
        NUM_HEADS = 16
        D_HEAD = D_MODEL // NUM_HEADS
        BATCH = 4
        SEQ = 256

        def _trunc_normal(key, shape, sd):
            return sd * jax.random.truncated_normal(key, -3.0, 3.0, shape, dtype=jnp.float32)
        key = jax.random.key(seed)
        kx, kq, kk, kv, ko = jax.random.split(key, 5)
        sd = (2.0 / (NUM_HEADS * D_HEAD + D_MODEL)) ** 0.5
        x = jax.random.normal(kx, (BATCH, SEQ, D_MODEL), dtype=jnp.float32)
        WQ = _trunc_normal(kq, (NUM_HEADS, D_HEAD, D_MODEL), sd)
        WK = _trunc_normal(kk, (NUM_HEADS, D_HEAD, D_MODEL), sd)
        WV = _trunc_normal(kv, (NUM_HEADS, D_HEAD, D_MODEL), sd)
        WO = _trunc_normal(ko, (NUM_HEADS, D_MODEL, D_HEAD), sd)
        return {'x': x, 'WQ': WQ, 'WK': WK, 'WV': WV, 'WO': WO}
    _L0_attn_a_in = _L0_attn_a_setup()

    def _L0_attn_b_setup():
        import jax, jax.numpy as jnp
        import numpy as np
        B, S, E, H = (2, 256, 128, 16)
        D = E // H

        def _rope(x):
            s, d = (x.shape[-2], x.shape[-1])
            inv_freq = 1.0 / 10000.0 ** (jnp.arange(0, d, 2, dtype=jnp.float32) / d)
            freqs = jnp.arange(s, dtype=jnp.float32)[:, None] * inv_freq[None, :]
            cos, sin = (jnp.cos(freqs), jnp.sin(freqs))
            x1, x2 = (x[..., 0::2], x[..., 1::2])
            o1 = x1 * cos - x2 * sin
            o2 = x2 * cos + x1 * sin
            return jnp.stack([o1, o2], axis=-1).reshape(x.shape)
        key = jax.random.key(seed)
        kx, kq, kk, kv, ko = jax.random.split(key, 5)
        std = 1.0 / np.sqrt(E)
        return {'x': jax.random.normal(kx, (B, S, E), dtype=jnp.float32), 'W_q': jax.random.normal(kq, (E, E), dtype=jnp.float32) * std, 'W_k': jax.random.normal(kk, (E, E), dtype=jnp.float32) * std, 'W_v': jax.random.normal(kv, (E, E), dtype=jnp.float32) * std, 'W_o': jax.random.normal(ko, (E, E), dtype=jnp.float32) * std}
    _L0_attn_b_in = _L0_attn_b_setup()

    def _L0_ffn_setup():
        import jax, jax.numpy as jnp
        import numpy as np
        DIM = 128

        def _reference_tuple_inner(x, W_r, W_k, W_v, mu_r, mu_k):
            B, T, C = x.shape
            x_prev = jnp.concatenate([jnp.zeros((B, 1, C), x.dtype), x[:, :-1, :]], axis=1)
            xr = mu_r * x + (1.0 - mu_r) * x_prev
            xk = mu_k * x + (1.0 - mu_k) * x_prev
            r = jax.nn.sigmoid(jnp.einsum('btc,dc->btd', xr, W_r))
            k = jnp.einsum('btc,dc->btd', xk, W_k)
            k_act = jnp.square(jax.nn.relu(k))
            out = r * jnp.einsum('btc,dc->btd', k_act, W_v)
            new_state = x[:, -1, :]
            return (out, new_state)
        key = jax.random.key(seed)
        ks = jax.random.split(key, 6)
        B, T, C = (8, 256, DIM)
        x = jax.random.normal(ks[0], (B, T, C), dtype=jnp.float32)
        s = 1.0 / np.sqrt(C)
        W_r = jax.random.uniform(ks[1], (C, C), jnp.float32, -s, s)
        W_k = jax.random.uniform(ks[2], (C, C), jnp.float32, -s, s)
        W_v = jax.random.uniform(ks[3], (C, C), jnp.float32, -s, s)
        mu_r = jax.random.uniform(ks[4], (C,), jnp.float32)
        mu_k = jax.random.uniform(ks[5], (C,), jnp.float32)
        return {'x': x, 'W_r': W_r, 'W_k': W_k, 'W_v': W_v, 'mu_r': mu_r, 'mu_k': mu_k}
    _L0_ffn_in = _L0_ffn_setup()
    _d = {'L0_attn_a_x': _L0_attn_a_in['x'], 'L0_attn_a_WQ': _L0_attn_a_in['WQ'], 'L0_attn_a_WK': _L0_attn_a_in['WK'], 'L0_attn_a_WV': _L0_attn_a_in['WV'], 'L0_attn_a_WO': _L0_attn_a_in['WO'], 'L0_attn_b_W_q': _L0_attn_b_in['W_q'], 'L0_attn_b_W_k': _L0_attn_b_in['W_k'], 'L0_attn_b_W_v': _L0_attn_b_in['W_v'], 'L0_attn_b_W_o': _L0_attn_b_in['W_o'], 'L0_ffn_W_r': _L0_ffn_in['W_r'], 'L0_ffn_W_k': _L0_ffn_in['W_k'], 'L0_ffn_W_v': _L0_ffn_in['W_v'], 'L0_ffn_mu_r': _L0_ffn_in['mu_r'], 'L0_ffn_mu_k': _L0_ffn_in['mu_k']}
    _x0 = _d['L0_attn_a_x']
    _d['L0_attn_a_x'] = jax.random.normal(jax.random.fold_in(jax.random.key(seed), 1), (8, 512, 128), dtype=_x0.dtype)
    del _x0
    return _d

def reference(L0_attn_a_x, L0_attn_a_WQ, L0_attn_a_WK, L0_attn_a_WV, L0_attn_a_WO, L0_attn_b_W_q, L0_attn_b_W_k, L0_attn_b_W_v, L0_attn_b_W_o, L0_ffn_W_r, L0_ffn_W_k, L0_ffn_W_v, L0_ffn_mu_r, L0_ffn_mu_k):

    def _L0_attn_a_ref(x, WQ, WK, WV, WO):
        import jax, jax.numpy as jnp
        import numpy as np
        import math
        D_MODEL = 128
        NUM_HEADS = 16
        D_HEAD = D_MODEL // NUM_HEADS
        BATCH = 4
        SEQ = 256

        def _trunc_normal(key, shape, sd):
            return sd * jax.random.truncated_normal(key, -3.0, 3.0, shape, dtype=jnp.float32)
        Q = jnp.einsum('bsd,hkd->bhsk', x, WQ)
        K = jnp.einsum('bsd,hkd->bhsk', x, WK)
        V = jnp.einsum('bsd,hkd->bhsk', x, WV)
        d_k = Q.shape[-1]
        scores = jnp.einsum('bhqd,bhkd->bhqk', Q, K) / math.sqrt(d_k)
        seq_len = x.shape[-2]
        causal = jnp.tril(jnp.ones((seq_len, seq_len), dtype=bool))
        scores = jnp.where(causal, scores, -jnp.inf)
        probs = jax.nn.softmax(scores, axis=-1)
        attn = jnp.einsum('bhqk,bhkv->bhqv', probs, V)
        return jnp.einsum('bhsv,hdv->bsd', attn, WO)

    def _L0_attn_b_ref(x, W_q, W_k, W_v, W_o):
        import jax, jax.numpy as jnp
        import numpy as np
        B, S, E, H = (2, 256, 128, 16)
        D = E // H

        def _rope(x):
            s, d = (x.shape[-2], x.shape[-1])
            inv_freq = 1.0 / 10000.0 ** (jnp.arange(0, d, 2, dtype=jnp.float32) / d)
            freqs = jnp.arange(s, dtype=jnp.float32)[:, None] * inv_freq[None, :]
            cos, sin = (jnp.cos(freqs), jnp.sin(freqs))
            x1, x2 = (x[..., 0::2], x[..., 1::2])
            o1 = x1 * cos - x2 * sin
            o2 = x2 * cos + x1 * sin
            return jnp.stack([o1, o2], axis=-1).reshape(x.shape)
        b, s, e = x.shape
        h, d = (H, e // H)
        q = (x @ W_q.T).reshape(b, s, h, d).transpose(0, 2, 1, 3)
        k = (x @ W_k.T).reshape(b, s, h, d).transpose(0, 2, 1, 3)
        v = (x @ W_v.T).reshape(b, s, h, d).transpose(0, 2, 1, 3)
        q = _rope(q)
        k = _rope(k)
        attn_scale = 1.0 / np.sqrt(e)
        scores = jnp.einsum('bhsd,bhtd->bhst', q, k) * attn_scale
        causal = jnp.triu(jnp.ones((s, s), dtype=bool), k=1)
        scores = jnp.where(causal, -jnp.inf, scores)
        probs = jax.nn.softmax(scores, axis=-1)
        out = jnp.einsum('bhst,bhtd->bhsd', probs, v)
        out = out.transpose(0, 2, 1, 3).reshape(b, s, e)
        return out @ W_o.T

    def _L0_ffn_ref(x, W_r, W_k, W_v, mu_r, mu_k):
        import jax, jax.numpy as jnp
        import numpy as np
        DIM = 128

        def _reference_tuple_inner(x, W_r, W_k, W_v, mu_r, mu_k):
            B, T, C = x.shape
            x_prev = jnp.concatenate([jnp.zeros((B, 1, C), x.dtype), x[:, :-1, :]], axis=1)
            xr = mu_r * x + (1.0 - mu_r) * x_prev
            xk = mu_k * x + (1.0 - mu_k) * x_prev
            r = jax.nn.sigmoid(jnp.einsum('btc,dc->btd', xr, W_r))
            k = jnp.einsum('btc,dc->btd', xk, W_k)
            k_act = jnp.square(jax.nn.relu(k))
            out = r * jnp.einsum('btc,dc->btd', k_act, W_v)
            new_state = x[:, -1, :]
            return (out, new_state)
        return _reference_tuple_inner(x, W_r, W_k, W_v, mu_r, mu_k)[0]
    x = L0_attn_a_x
    x = x + _L0_attn_a_ref(_layernorm(x, axis=-1), L0_attn_a_WQ, L0_attn_a_WK, L0_attn_a_WV, L0_attn_a_WO)
    x = x + _L0_ffn_ref(_layernorm(x, axis=-1), L0_ffn_W_r, L0_ffn_W_k, L0_ffn_W_v, L0_ffn_mu_r, L0_ffn_mu_k)
    x = x + _L0_attn_b_ref(_layernorm(x, axis=-1), L0_attn_b_W_q, L0_attn_b_W_k, L0_attn_b_W_v, L0_attn_b_W_o)
    x = x + _L0_ffn_ref(_layernorm(x, axis=-1), L0_ffn_W_r, L0_ffn_W_k, L0_ffn_W_v, L0_ffn_mu_r, L0_ffn_mu_k)
    return x

_drawn_inputs = setup_inputs


def setup_inputs(seed=0):
    import zlib

    import numpy as np

    out = dict(_drawn_inputs(seed))
    spreads = {}
    factors = {'L0_ffn_mu_r': 3.243}
    for name, (base, spread) in spreads.items():
        noise = np.random.default_rng([zlib.crc32(name.encode()), seed]).standard_normal(out[name].shape)
        drawn = base * np.exp(spread * noise) if base else spread * noise
        out[name] = jnp.asarray(drawn.astype(out[name].dtype))
    for name, factor in factors.items():
        out[name] = (out[name] * factor).astype(out[name].dtype)
    return out
```

```python
from contextlib import ExitStack

import concourse.bass as bass
from concourse import mybir

F32 = mybir.dt.float32
BF16 = mybir.dt.bfloat16
ALU = mybir.AluOpType
ACT = mybir.ActivationFunctionType
AX = mybir.AxisListType

P = 128
BATCH, SEQ, DM = 8, 512, 128
HEADS, DH = 16, 8
LAYERS = 2
UNITS = LAYERS * BATCH
TILES = SEQ // P
GROUPS, GH = 4, 4
SLOTS = GROUPS
PARTS = 3
Q_TERMS = [0, 0, 0, 1, 1, 2]
K_TERMS = [0, 1, 2, 0, 1, 0]
TERM_RUNS = [(0, 0, 3, 0, 0), (0, 3, 2, 1, 0), (0, 5, 1, 2, 0), (1, 0, 3, 0, 1), (1, 3, 2, 0, 1), (1, 5, 1, 0, 0)]
TERM_ROWS = DH * len(Q_TERMS)
AUG_ROWS = TERM_ROWS + PARTS
HALF = 64
OW = 32
EPS = 1e-5
MASKED = -3.0e38

P1_UNITS = 12
P2_UNITS = 6
P1_LIST = [(0, [0, 2]), (0, [1, 3]), (1, [0, 2]), (1, [1, 3])] + [(2, [j]) for j in range(4)] + [(3, [j]) for j in range(4)]
P2_LIST = [(0, [0]), (0, [1]), (1, [0]), (1, [1]), (2, [0, 1]), (3, [0, 1])]
P2_UP_TO = [2, 4, 5, 6]
P_OFF = [0, 512, 896, 1152]
P_LEN = 1280

P2_AT = {0: 0, 2: 1, 4: 2, 6: 3, 8: 4, 9: 5}
PV_AT = {1: 0, 3: 1, 5: 2, 7: 3}
ROUNDS = [
    [(0, "attn_t", -2, 0), (2, "max_t", -1, 3), (4, "oproj", -2, 0), (7, "xn_t", 1, 0)],
    [(1, "max_t", 0, 0), (3, "qproj", 1, 0), (5, "kproj", 1, 0), (8, "fx_t", -2, 0)],
    [(1, "max_t", 0, 1), (5, "fk", -2, 0), (7, "fr", -2, 0)],
    [(0, "onat", -1, 0), (1, "max_t", 0, 2), (3, "onat", -1, 1), (4, "onat", -1, 2), (5, "onat", -1, 3),
     (7, "fv", -2, 0), (9, "vproj", 1, 0)],
]
PER_UNIT = {"attn_t": 1, "max_t": 4, "oproj": 1, "xn_t": 1, "qproj": 1, "kproj": 1, "fx_t": 1, "fk": 1,
            "fr": 1, "onat": 4, "fv": 1, "vproj": 1}
FIRST_BODY, LOOP_FROM, LOOP_TO, LAST_BODY = -1, 2, UNITS - 1, UNITS + 1


def active(v):
    return not isinstance(v, int) or 0 <= v < UNITS


def layer_of(v):
    return v // BATCH if isinstance(v, int) else (v >> 3).with_bounds(min_val=0, max_val=LAYERS - 1)


def max_group(u, s):
    return (u, s - 1) if s >= 1 else (u - 1, 3)


def pass2_group(u, s):
    return (u, s - 2) if s >= 2 else (u - 1, s + 2)


def pv_group(u, s):
    return (u, 0) if s == 3 else (u - 1, s + 1)


def build(nc, x_d, w_d, wf_d, mu_d, rope_d, out_d):
    with ExitStack() as ctx:
        def sb(name, shape, dt=F32):
            return ctx.enter_context(nc.sbuf_tensor(name, shape, dt))

        def ps(name, shape):
            return ctx.enter_context(nc.psum_tensor(name, shape, F32))

        def sem(name):
            return ctx.enter_context(nc.semaphore(name))

        x_sb = sb("x_sb", [P, UNITS * SEQ])
        w_all = sb("w_all", [P, LAYERS * 4 * DM])
        w_qkv = sb("w_qkv", [P, 3 * DM])
        w_o = sb("w_o", [P, DM])
        w_ffn = sb("w_ffn", [P, 3 * DM])
        mu = sb("mu", [P, 2])
        rope = sb("rope", [P, LAYERS * 2 * 2 * SEQ])
        ident = sb("ident", [P, P])
        ident_b = sb("ident_b", [P, P], BF16)
        causal = sb("causal", [P, GH * P], BF16)
        eps_t = sb("eps_t", [P, TILES])
        mhalf = sb("mhalf", [P, TILES])
        bn = [sb(f"bn{i}", [P, TILES, 6]) for i in range(2)]
        mv = [sb(f"mv{i}", [P, TILES, 2]) for i in range(2)]
        ve = [sb(f"ve{i}", [P, TILES]) for i in range(2)]
        rstd = [sb(f"rstd{i}", [P, TILES]) for i in range(2)]
        xn = [sb(f"xn{i}", [P, SEQ]) for i in range(2)]
        xn_t = sb("xn_t", [P, SEQ])
        qk = sb("qk", [P, 2 * SEQ])
        qk_sw = sb("qk_sw", [P, 2 * SEQ])
        qk_rot = sb("qk_rot", [P, 2 * SEQ])
        qk_rest = sb("qk_rest", [P, 2 * SEQ])
        parts = sb("parts", [P, PARTS, 2, SEQ], BF16)
        aug = sb("aug", [P, 2, HEADS // 2, SEQ], BF16)
        v_nat = sb("v_nat", [P, TILES, HEADS, DH])
        v_aug = sb("v_aug", [P, TILES, HEADS, OW])
        nmax = [sb(f"nmax{i}", [P, TILES, 2, 2]) for i in range(2)]
        nmax_r = sb("nmax_r", [P, TILES, 2, 2])
        nmax_p = sb("nmax_p", [P, TILES, 2, 2, PARTS], BF16)
        nmax_t = sb("nmax_t", [2 * PARTS * 2, SEQ], BF16)
        probs = [sb(f"probs{i}", [P, GH, P_LEN]) for i in range(2)]
        o_t = sb("o_t", [P, GROUPS, SEQ])
        rsum = sb("rsum", [P, TILES, HEADS])
        attn = sb("attn", [P, TILES, HEADS, DH])
        attn_t = sb("attn_t", [P, SEQ])
        x_mid = sb("x_mid", [P, SEQ])
        fx = sb("fx", [P, 1 + SEQ])
        fd = sb("fd", [P, SEQ])
        f_xk = sb("f_xk", [P, SEQ])
        f_xr = sb("f_xr", [P, SEQ])
        k_relu = sb("k_relu", [P, SEQ])
        k_sq = sb("k_sq", [P, SEQ])
        gate = sb("gate", [P, SEQ])
        gate1 = sb("gate1", [P, SEQ])
        gated = sb("gated", [P, SEQ])

        terms_d = nc.dram_tensor("terms", (2, len(Q_TERMS), P, SEQ), BF16).ap()

        p1 = ps("p1", [P, 2, 512])
        p2 = [ps(f"p2_{i}", [P, 2, 512]) for i in range(2)]
        pv = ps("pv", [P, 512])
        shared = ps("shared", [P, 512])
        shared_b = shared[:, :].bitcast(BF16)

        x_in = [sem(f"x_in{i}") for i in range(3)]
        const_in = sem("const_in")
        setup = sem("setup")
        x_ready = sem("x_ready")
        w_in, wo_in, swap_in = sem("w_in"), sem("wo_in"), sem("swap_in")
        aug_in = [sem(f"aug_in{g}") for g in range(GROUPS)]
        terms_out = sem("terms_out")
        max_in = [sem(f"max_in{g}") for g in range(GROUPS)]
        made = {n: sem(f"made_{n}") for n in PER_UNIT}
        taken = {n: sem(f"taken_{n}") for n in PER_UNIT}
        ln_stat = [sem(f"ln_stat{i}") for i in range(2)]
        ln_mv = [sem(f"ln_mv{i}") for i in range(2)]
        ln_ve = [sem(f"ln_ve{i}") for i in range(2)]
        ln_rstd = [sem(f"ln_rstd{i}") for i in range(2)]
        ln_done = [sem(f"ln_done{i}") for i in range(2)]
        rope_c, rope_s, rope_done = sem("rope_c"), sem("rope_s"), sem("rope_done")
        part0, rest0, part1, part2 = sem("part0"), sem("rest0"), sem("part1"), sem("part2")
        v_copied = sem("v_copied")
        p1_full, p1_max = sem("p1_full"), sem("p1_max")
        max_p = sem("max_p")
        p2_full, exp_done, mask_done = sem("p2_full"), sem("exp_done"), sem("mask_done")
        pv_full, o_out = sem("pv_full"), sem("o_out")
        rsum_done = sem("rsum_done")
        f_diff, f_xk_done, f_xr_done, sq_done = sem("f_diff"), sem("f_xk_done"), sem("f_xr_done"), sem("sq_done")
        gate_done, gated_done = sem("gate_done"), sem("gated_done")
        out_done = sem("out_done")
        SETUP = 12

        block = ctx.enter_context(nc.Block())

        def due(eng, count):
            if isinstance(count, int):
                return max(count, 0)
            value = eng.snap(eng.to_reg(count))
            eng.wait_ge(setup, SETUP)
            return value

        def bank_before(u, s, step):
            order = [(ss, st, n, du, k) for ss in range(SLOTS) for st, n, du, k in ROUNDS[ss]]
            at = [(ss, st) for ss, st, *_ in order].index((s, step))
            for back in range(1, 3 * len(order)):
                i = at - back
                body = i // len(order)
                _, _, n, du, k = order[i % len(order)]
                v = u + (body + du)
                if isinstance(v, int) and v < 0 and u + body < FIRST_BODY:
                    return None
                if active(v):
                    return taken[n], v * PER_UNIT[n] + (k + 1)
            return None

        def run(eng, body):
            for u in range(FIRST_BODY, LOOP_FROM):
                body(u)
            with eng.Fori(LOOP_FROM, LOOP_TO) as u:
                body(u)
            for u in range(LOOP_TO, LAST_BODY + 1):
                body(u)

        @block.sync
        def _(sp):
            sp.dma_start(w_all[:, :], w_d).then_inc(const_in, 16)
            xr = x_d.rearrange("b (t p) d -> b p t d", p=P)

            def load_x(b, s):
                sp.dma_start(x_sb[:, b * SEQ:(b + 1) * SEQ].rearrange("p (t d) -> p t d", d=DM), xr[b]).then_inc(s, 16)

            load_x(0, x_in[0])
            load_x(1, x_in[1])
            sp.dma_start(rope[:, :], rope_d).then_inc(const_in, 16)
            sp.dma_start(w_ffn[:, :], wf_d).then_inc(const_in, 16)
            sp.dma_start(mu[:, :], mu_d).then_inc(const_in, 16)
            sp.wait_ge(const_in, 64)
            for b in range(2, BATCH):
                load_x(b, x_in[2])
            sp.wait_ge(setup, SETUP)

            def load_w(v):
                if not active(v):
                    return
                sp.wait_ge(made["vproj"], due(sp, v))
                layer = layer_of(v)
                sp.dma_start(w_qkv[:, :], w_all[:, bass.ds(layer * (4 * DM), 3 * DM)]).then_inc(w_in, 16)

            def load_wo(v):
                if not active(v):
                    return
                sp.wait_ge(made["oproj"], due(sp, v))
                layer = layer_of(v)
                sp.dma_start(w_o[:, :], w_all[:, bass.ds(layer * (4 * DM) + 3 * DM, DM)]).then_inc(wo_in, 16)

            def swap(v):
                if not active(v):
                    return
                sp.wait_ge(taken["qproj"], due(sp, v + 1))
                sp.wait_ge(taken["kproj"], due(sp, v + 1))
                sp.wait_ge(rope_s, due(sp, v))
                for k in range(2):
                    a, b = slice(k * HALF, (k + 1) * HALF), slice((1 - k) * HALF, (2 - k) * HALF)
                    sp.dma_start(qk_sw[a, :], qk[b, :]).then_inc(swap_in, 16)

            def send_terms(v):
                if not active(v):
                    return
                sp.wait_ge(part0, due(sp, v + 1))
                sp.wait_ge(part1, due(sp, v + 1))
                sp.wait_ge(part2, due(sp, v + 1))
                for g in range(GROUPS):
                    sp.wait_ge(aug_in[g], due(sp, v * 32))
                for side, t0, n, part, step in TERM_RUNS:
                    src = parts[:, part, side, :].unsqueeze(1).broadcast_to([P, n, SEQ]) if step == 0 \
                        else parts[:, part:part + n, side, :]
                    sp.dma_start(terms_d[side, t0:t0 + n].rearrange("t p n -> p t n"), src).then_inc(terms_out, 16)

            def fetch_terms(v, g):
                if not active(v):
                    return
                sp.wait_ge(terms_out, due(sp, (v + 1) * (16 * len(TERM_RUNS))))
                sp.wait_ge(p2_full, due(sp, (v - 1) * (P2_UNITS * GROUPS) + P2_UNITS * (g + 1)))
                src = terms_d.rearrange("s t (d par pair) n -> par (t d) s pair n", par=2, d=DH)
                for par in range(2):
                    sp.dma_start(aug[HALF * par:HALF * par + TERM_ROWS, :, 2 * g:2 * g + 2, :],
                                 src[par][:, :, 2 * g:2 * g + 2, :]).then_inc(aug_in[g], 16)

            def put_max(v, g):
                if not active(v):
                    return
                sp.wait_ge(taken["max_t"], due(sp, v * 4 + (g + 1)))
                for par in range(2):
                    row = HALF * par + TERM_ROWS
                    for jj in range(2):
                        src = nmax_t[6 * par + 3 * jj:6 * par + 3 * jj + PARTS, :]
                        sp.dma_start(aug[row:row + PARTS, 0, 2 * g + jj, :], src).then_inc(max_in[g], 16)

            def body(u):
                load_w(u + 1)
                fetch_terms(u, 1)
                put_max(u - 1, 3)
                fetch_terms(u, 2)
                put_max(u, 0)
                swap(u + 1)
                fetch_terms(u, 3)
                put_max(u, 1)
                load_wo(u - 1)
                put_max(u, 2)
                send_terms(u + 1)
                fetch_terms(u + 1, 0)

            run(sp, body)
            orr = out_d.rearrange("b (t p) d -> b p t d", p=P)
            for b in range(BATCH):
                sp.wait_ge(x_ready, 2 * BATCH + b + 1)
                sp.dma_start(orr[b], x_sb[:, b * SEQ:(b + 1) * SEQ].rearrange("p (t d) -> p t d", d=DM)).then_inc(out_done, 16)
            sp.wait_ge(out_done, 16 * BATCH)

        @block.tensor
        def _(pe):
            pe.wait_ge(setup, SETUP)
            pe.wait_ge(const_in, 64)

            def pass1(u, g, i):
                if not active(u):
                    return
                if i == 0:
                    pe.wait_ge(aug_in[g], due(pe, (u + 1) * 32))
                n = GROUPS * P1_UNITS
                pe.wait_ge(p1_max, due(pe, u * n + (P1_UNITS * g + i - 1)))
                bank = (P1_UNITS * g + i) % 2
                qt, heads = P1_LIST[i]
                length = (qt + 1) * P
                out = p1[:, bank, 0:len(heads) * length].rearrange("p (h k) -> p h k", h=len(heads))
                pe.matmul(out[:, :, qt * P:length], ident_b[:, :],
                          causal[:, 0:len(heads) * P].rearrange("p (h k) -> p h k", h=len(heads)),
                          start=True, stop=False, skip_group_check=True)
                for n_, j in enumerate(heads):
                    row, pair = HALF * (j % 2), 2 * g + j // 2
                    last = pe.matmul(out[:, n_, :], aug[row:row + TERM_ROWS, 0, pair, qt * P:(qt + 1) * P],
                                     aug[row:row + TERM_ROWS, 1, pair, 0:length],
                                     start=False, stop=True, skip_group_check=True)
                last.then_inc(p1_full, 1)

            def pass2(v, g, i):
                if not active(v):
                    return
                if i == 0:
                    pe.wait_ge(max_in[g], due(pe, (v + 1) * (16 * 4)))
                n = GROUPS * P2_UNITS
                pe.wait_ge(exp_done, due(pe, v * n + (P2_UNITS * g + i - 1)))
                kt, pairs = P2_LIST[i]
                width = SEQ - kt * P
                for m, jj in enumerate(pairs):
                    for par in range(2):
                        row, pair = HALF * par, 2 * g + jj
                        last = pe.matmul(p2[i % 2][:, par, m * width:(m + 1) * width],
                                         aug[row:row + AUG_ROWS, 1, pair, kt * P:(kt + 1) * P],
                                         aug[row:row + AUG_ROWS, 0, pair, kt * P:SEQ], start=True, stop=True)
                last.then_inc(p2_full, 1)

            def times_v(v, g, kt):
                if not active(v):
                    return
                if kt == 0:
                    pe.wait_ge(v_copied, due(pe, v * 4 + (g + 1)))
                    pe.wait_ge(o_out, due(pe, v * 4 + g))
                pe.wait_ge(mask_done, due(pe, v * 16 + (4 * g + kt + 1)))
                for j in range(GH):
                    last = pe.matmul(pv[OW * j:OW * (j + 1), kt * P:SEQ], v_aug[:, kt, GH * g + j, :],
                                     probs[g % 2][:, j, P_OFF[kt]:P_OFF[kt] + SEQ - kt * P],
                                     start=(kt == 0), stop=(kt == TILES - 1), tile_position=(0, OW * j))
                if kt == TILES - 1:
                    last.then_inc(pv_full, 1)

            def tile_t(i):
                return slice(i * P, (i + 1) * P)

            def shared_round(u, s, step, name, dv, k):
                v = u + dv
                if not active(v):
                    return
                before = bank_before(u, s, step)
                if before:
                    pe.wait_ge(before[0], due(pe, before[1]))
                if name == "xn_t":
                    pe.wait_ge(ln_done[0], due(pe, v + 1))
                    for t in range(TILES):
                        last = pe.transpose(shared[:, tile_t(t)], xn[0][:, tile_t(t)], ident[:, :])
                elif name in ("qproj", "kproj"):
                    pe.wait_ge(taken["xn_t"], due(pe, v + 1))
                    pe.wait_ge(w_in, due(pe, (v + 1) * 16))
                    w = 0 if name == "qproj" else 1
                    last = pe.matmul(shared[:, :], w_qkv[:, tile_t(w)], xn_t[:, :], start=True, stop=True)
                elif name == "vproj":
                    for t in range(TILES):
                        last = pe.matmul(shared[:, tile_t(t)], xn_t[:, tile_t(t)], w_qkv[:, tile_t(2)], start=True, stop=True)
                elif name == "max_t":
                    pe.wait_ge(max_p, due(pe, v * 16 + (4 * k + 4)))
                    for t in range(TILES):
                        last = pe.transpose(shared_b[0:4 * PARTS, tile_t(t)],
                                            nmax_p[:, t, :, :, :].rearrange("p a b k -> p (a b k)"), ident_b[:, :])
                elif name == "onat":
                    pe.wait_ge(o_out, due(pe, v * 4 + 4))
                    for g in range(GROUPS):
                        last = pe.transpose(shared[:, tile_t(g)], o_t[:, g, tile_t(k)], ident[:, :])
                elif name == "attn_t":
                    for t in range(TILES):
                        last = pe.transpose(shared[:, tile_t(t)], attn[:, t, :, :].rearrange("p h d -> p (h d)"), ident[:, :])
                elif name == "oproj":
                    pe.wait_ge(taken["attn_t"], due(pe, v + 1))
                    pe.wait_ge(wo_in, due(pe, (v + 1) * 16))
                    for t in range(TILES):
                        last = pe.matmul(shared[:, tile_t(t)], attn_t[:, tile_t(t)], w_o[:, :], start=True, stop=True)
                elif name == "fx_t":
                    pe.wait_ge(ln_done[1], due(pe, v + 1))
                    for t in range(TILES):
                        last = pe.transpose(shared[:, tile_t(t)], xn[1][:, tile_t(t)], ident[:, :])
                elif name == "fk":
                    pe.wait_ge(f_xk_done, due(pe, v + 1))
                    last = pe.matmul(shared[:, :], w_ffn[:, tile_t(1)], f_xk[:, :], start=True, stop=True)
                elif name == "fr":
                    pe.wait_ge(f_xr_done, due(pe, v + 1))
                    for t in range(TILES):
                        last = pe.matmul(shared[:, tile_t(t)], f_xr[:, tile_t(t)], w_ffn[:, tile_t(0)], start=True, stop=True)
                elif name == "fv":
                    pe.wait_ge(sq_done, due(pe, v + 1))
                    for t in range(TILES):
                        last = pe.matmul(shared[:, tile_t(t)], k_sq[:, tile_t(t)], w_ffn[:, tile_t(2)], start=True, stop=True)
                last.then_inc(made[name], 1)

            def body(u):
                for s in range(SLOTS):
                    for i in range(P1_UNITS):
                        pass1(u, s, i)
                        if i in P2_AT:
                            pass2(*pass2_group(u, s), P2_AT[i])
                        if i in PV_AT:
                            times_v(*pv_group(u, s), PV_AT[i])
                        for step, name, dv, k in ROUNDS[s]:
                            if step == i:
                                shared_round(u, s, step, name, dv, k)

            run(pe, body)

        @block.scalar
        def _(act):
            act.wait_ge(setup, SETUP)

            def exps(v, g, i):
                if not active(v):
                    return
                if i == 0:
                    act.wait_ge(pv_full, due(act, v * 4 + (g - 1)))
                act.wait_ge(p2_full, due(act, v * (GROUPS * P2_UNITS) + (P2_UNITS * g + i + 1)))
                kt, pairs = P2_LIST[i]
                width = SEQ - kt * P
                if len(pairs) == 1:
                    src = p2[i % 2][:, :, 0:width]
                    dst = probs[g % 2][:, 2 * pairs[0]:2 * pairs[0] + 2, P_OFF[kt]:P_OFF[kt] + width]
                else:
                    src = p2[i % 2][:, :, 0:2 * width].rearrange("p par (jj q) -> p par jj q", jj=2)
                    dst = probs[g % 2][:, :, P_OFF[kt]:P_OFF[kt] + width].rearrange("p (jj par) q -> p par jj q", par=2)
                act.activation(dst, src, ACT.Exp).then_inc(exp_done, 1)

            def out_copy(v, g):
                if not active(v):
                    return
                act.wait_ge(made["onat"], due(act, v * 4))
                act.wait_ge(pv_full, due(act, v * 4 + (g + 1)))
                act.copy(o_t[:, g, :], pv[:, :]).then_inc(o_out, 1)

            def take(v, name, k):
                if not active(v) or name in ("onat", "oproj", "fv"):
                    return
                if name == "xn_t":
                    act.wait_ge(made["vproj"], due(act, v))
                    act.wait_ge(made["xn_t"], due(act, v + 1))
                    act.copy(xn_t[:, :], shared[:, :]).then_inc(taken[name], 1)
                elif name in ("qproj", "kproj"):
                    side = 0 if name == "qproj" else 1
                    act.wait_ge(swap_in, due(act, v * 32))
                    act.wait_ge(rope_c, due(act, v))
                    act.wait_ge(made[name], due(act, v + 1))
                    act.copy(qk[:, side * SEQ:(side + 1) * SEQ], shared[:, :]).then_inc(taken[name], 1)
                elif name == "vproj":
                    act.wait_ge(v_copied, due(act, v * 4))
                    act.wait_ge(made[name], due(act, v + 1))
                    act.copy(v_nat[:, :, :, :].rearrange("p t h d -> p (t h d)"), shared[:, :]).then_inc(taken[name], 1)
                elif name == "max_t":
                    w, k0 = (v, k - 1) if k else (v - 1, 3)
                    if active(w):
                        act.wait_ge(max_in[k0], due(act, (w + 1) * (16 * 4)))
                    act.wait_ge(made[name], due(act, v * 4 + (k + 1)))
                    act.copy(nmax_t[:, :], shared_b[0:4 * PARTS, 0:SEQ]).then_inc(taken[name], 1)
                elif name == "attn_t":
                    act.wait_ge(made["oproj"], due(act, v))
                    act.wait_ge(made[name], due(act, v + 1))
                    act.copy(attn_t[:, :], shared[:, :]).then_inc(taken[name], 1)
                elif name == "fx_t":
                    act.wait_ge(f_xk_done, due(act, v))
                    act.wait_ge(f_xr_done, due(act, v))
                    act.wait_ge(made[name], due(act, v + 1))
                    act.copy(fx[:, 1:1 + SEQ], shared[:, :]).then_inc(taken[name], 1)
                elif name == "fk":
                    act.wait_ge(sq_done, due(act, v))
                    act.wait_ge(made[name], due(act, v + 1))
                    act.activation(k_relu[:, :], shared[:, :], ACT.Relu).then_inc(taken[name], 1)
                elif name == "fr":
                    act.wait_ge(gate_done, due(act, v))
                    act.wait_ge(made[name], due(act, v + 1))
                    act.activation(gate[:, :], shared[:, :], ACT.Tanh, scale=0.5).then_inc(taken[name], 1)

            def body(u):
                for s in range(SLOTS):
                    for i in range(P1_UNITS):
                        if i in P2_AT:
                            exps(*pass2_group(u, s), P2_AT[i])
                        for step, name, dv, k in ROUNDS[s]:
                            if step == i:
                                take(u + dv, name, k)
                        if i == 7:
                            out_copy(*pv_group(u, s))

            run(act, body)

        @block.vector
        def _(dve):
            dve.memset(v_aug[:, :, :, :], 1.0).then_inc(setup, 1)
            dve.memset(aug[:, :, :, :], 1.0).then_inc(setup, 1)
            dve.memset(fx[:, 0:1], 0.0).then_inc(setup, 1)
            dve.memset(eps_t[:, :], EPS).then_inc(setup, 1)
            dve.memset(mhalf[:, :], -0.5).then_inc(setup, 1)
            dve.wait_ge(x_in[0], 16)
            dve.sem_inc(x_ready, BATCH)
            dve.wait_ge(setup, SETUP)

            def x_at(v):
                if isinstance(v, int):
                    return x_sb[:, (v % UNITS) * SEQ:(v % UNITS + 1) * SEQ]
                return x_sb[:, bass.ds((v % UNITS) * SEQ, SEQ)]

            def row_max(u, g, i):
                if not active(u):
                    return
                if i == 0:
                    w, g0 = (u, g - 2) if g >= 2 else (u - 1, g + 2)
                    if active(w):
                        dve.wait_ge(max_p, due(dve, w * 16 + (4 * g0 + 3)))
                dve.wait_ge(p1_full, due(dve, u * (GROUPS * P1_UNITS) + (P1_UNITS * g + i + 1)))
                qt, heads = P1_LIST[i]
                length = (qt + 1) * P
                src = p1[:, (P1_UNITS * g + i) % 2, 0:len(heads) * length].rearrange("p (h k) -> p h k", h=len(heads))
                jj, par = heads[0] // 2, heads[0] % 2
                if len(heads) == 2:
                    dst = nmax[g % 2][:, qt, par, :]
                else:
                    dst = nmax[g % 2][:, qt, par, jj:jj + 1]
                dve.tensor_reduce(dst, src, AX.X, ALU.max, negate=True).then_inc(p1_max, 1)

            def stats(v, which, x):
                if not active(v):
                    return
                for t in range(TILES):
                    last = dve.bn_stats(bn[which][:, t, :], x[:, t * P:(t + 1) * P])
                last.then_inc(ln_stat[which], 1)
                dve.wait_ge(ln_stat[which], due(dve, v + 1))
                for t in range(TILES):
                    last = dve.bn_aggr(mv[which][:, t, :], bn[which][:, t, :])
                last.then_inc(ln_mv[which], 1)

            def normalise(v, which, x):
                if not active(v):
                    return
                dve.wait_ge(ln_rstd[which], due(dve, v + 1))
                dve.wait_ge(made["xn_t" if which == 0 else "fx_t"], due(dve, v))
                for t in range(TILES):
                    last = dve.tensor_scalar(xn[which][:, t * P:(t + 1) * P], x[:, t * P:(t + 1) * P],
                                             mv[which][:, t, 0:1], rstd[which][:, t:t + 1], ALU.subtract, ALU.mult)
                last.then_inc(ln_done[which], 1)

            def first_stats(v):
                if not active(v):
                    return
                if isinstance(v, int) and v < 3:
                    dve.wait_ge(x_in[v], 16 if v < 2 else 16 * (BATCH - 2))
                dve.wait_ge(x_ready, due(dve, v + 1))
                stats(v, 0, x_at(v))

            def cast_part(v, k):
                if not active(v):
                    return
                if k == 0:
                    dve.wait_ge(terms_out, due(dve, v * (16 * len(TERM_RUNS))))
                    dve.wait_ge(rope_done, due(dve, v + 1))
                    dve.tensor_copy(parts[:, 0, :, :].rearrange("p a n -> p (a n)"), qk_rot[:, :]).then_inc(part0, 1)
                else:
                    dve.wait_ge(rest0, due(dve, v + 1))
                    dve.tensor_copy(parts[:, 1, :, :].rearrange("p a n -> p (a n)"), qk_rest[:, :]).then_inc(part1, 1)

            def divide(v, k):
                if not active(v):
                    return
                if k == 0:
                    dve.wait_ge(made["attn_t"], due(dve, v))
                dve.wait_ge(made["onat"], due(dve, v * 4 + (k + 1)))
                o = shared[:, :].rearrange("p (h c) -> p h c", c=OW)
                dve.reciprocal(rsum[:, k, :], o[:, :, DH]).then_inc(rsum_done, 1)
                dve.wait_ge(rsum_done, due(dve, v * 4 + (k + 1)))
                dve.tensor_tensor(attn[:, k, :, :], o[:, :, 0:DH],
                                  rsum[:, k, :].unsqueeze(2).broadcast_to([P, HEADS, DH]), ALU.mult)\
                    .then_inc(taken["onat"], 1)

            def add_attn(v):
                if not active(v):
                    return
                dve.wait_ge(made["oproj"], due(dve, v + 1))
                dve.wait_ge(x_ready, due(dve, v + BATCH))
                dve.tensor_tensor(x_mid[:, :], shared[:, :], x_at(v), ALU.add).then_inc(taken["oproj"], 1)

            def mix(v, k):
                if not active(v):
                    return
                dst, done, reader = ((f_xr, f_xr_done, "fr"), (f_xk, f_xk_done, "fk"))[k]
                dve.wait_ge(made[reader], due(dve, v))
                dve.wait_ge(f_diff, due(dve, v + 1))
                dve.scalar_tensor_tensor(out=dst[:, :], in0=fd[:, :], scalar=mu[:, k:k + 1], in1=fx[:, 0:SEQ],
                                         op0=ALU.mult, op1=ALU.add).then_inc(done, 1)

            def finish(v):
                if not active(v):
                    return
                dve.wait_ge(taken["fr"], due(dve, v + 1))
                dve.tensor_scalar(gate1[:, :], gate[:, :], 0.5, 0.5, ALU.mult, ALU.add).then_inc(gate_done, 1)
                dve.wait_ge(gate_done, due(dve, v + 1))
                dve.wait_ge(made["fv"], due(dve, v + 1))
                dve.tensor_tensor(gated[:, :], shared[:, :], gate1[:, :], ALU.mult).then_inc(taken["fv"], 1)
                dve.wait_ge(taken["fv"], due(dve, v + 1))
                dve.tensor_tensor(x_at(v + BATCH), gated[:, :], x_mid[:, :], ALU.add).then_inc(x_ready, 1)

            def body(u):
                for s in range(SLOTS):
                    for i in range(P1_UNITS):
                        row_max(u, s, i)
                        if s == 0:
                            if i == 1:
                                first_stats(u + 1)
                            if i == 3 and active(u + 1):
                                normalise(u + 1, 0, x_at(u + 1))
                            if i == 5:
                                add_attn(u - 2)
                            if i == 6 and active(u - 2):
                                dve.wait_ge(taken["oproj"], due(dve, (u - 2) + 1))
                                stats(u - 2, 1, x_mid)
                            if i == 9:
                                normalise(u - 2, 1, x_mid)
                        if s == 2:
                            if i == 1:
                                mix(u - 2, 1)
                            if i == 3:
                                mix(u - 2, 0)
                            if i == 7:
                                cast_part(u + 1, 0)
                        if s == 3:
                            if i == 2:
                                cast_part(u + 1, 1)
                            for step, name, dv, k in ROUNDS[s]:
                                if step == i and name == "onat":
                                    divide(u + dv, k)
                            if i == 8:
                                finish(u - 2)

            run(dve, body)

        @block.gpsimd
        def _(pool):
            pool.memset(ident[:, :], 0.0).then_inc(setup, 1)
            pool.memset(ident_b[:, :], 0.0).then_inc(setup, 1)
            pool.memset(causal[:, :], 0.0).then_inc(setup, 1)
            pool.wait_ge(setup, 8)
            pool.affine_select(out=ident[:, :], in_=ident[:, :], compare_op=ALU.not_equal, fill=1.0, base=0,
                               pattern=[[-1, P]], channel_multiplier=1).then_inc(setup, 1)
            pool.affine_select(out=ident_b[:, :], in_=ident_b[:, :], compare_op=ALU.not_equal, fill=1.0, base=0,
                               pattern=[[-1, P]], channel_multiplier=1).then_inc(setup, 1)
            pool.affine_select(out=causal[:, :].rearrange("p (h k) -> p h k", h=GH),
                               in_=causal[:, :].rearrange("p (h k) -> p h k", h=GH), compare_op=ALU.is_ge,
                               fill=MASKED, base=0, pattern=[[0, GH], [-1, P]], channel_multiplier=1)\
                .then_inc(setup, 1)
            pool.wait_ge(const_in, 64)
            pool.sem_inc(setup, 1)
            pool.wait_ge(setup, SETUP)

            def copy(out, in_):
                return pool.tensor_copy(out, in_)

            def split_max(v, g):
                if not active(v):
                    return
                src, at = nmax[g % 2], v * 16 + 4 * g
                w, g0 = (v, g - 1) if g else (v - 1, 3)
                if active(w):
                    pool.wait_ge(made["max_t"], due(pool, w * 4 + (g0 + 1)))
                pool.wait_ge(p1_max, due(pool, v * (GROUPS * P1_UNITS) + P1_UNITS * (g + 1)))
                copy(nmax_p[:, :, :, :, 0], src[:, :, :, :]).then_inc(max_p, 1)
                pool.wait_ge(max_p, due(pool, at + 1))
                pool.tensor_tensor(nmax_r[:, :, :, :], src[:, :, :, :], nmax_p[:, :, :, :, 0], ALU.subtract).then_inc(max_p, 1)
                pool.wait_ge(max_p, due(pool, at + 2))
                copy(nmax_p[:, :, :, :, 1], nmax_r[:, :, :, :]).then_inc(max_p, 1)
                pool.wait_ge(max_p, due(pool, at + 3))
                pool.tensor_tensor(nmax_p[:, :, :, :, 2], nmax_r[:, :, :, :], nmax_p[:, :, :, :, 1], ALU.subtract)\
                    .then_inc(max_p, 1)

            def mask(v, g, kt):
                if not active(v):
                    return
                pool.wait_ge(exp_done, due(pool, v * (GROUPS * P2_UNITS) + (P2_UNITS * g + P2_UP_TO[kt])))
                blk = probs[g % 2][:, :, P_OFF[kt]:P_OFF[kt] + P]
                pool.affine_select(out=blk, in_=blk, compare_op=ALU.is_ge, fill=0.0, base=0,
                                   pattern=[[0, GH], [1, P]], channel_multiplier=-1).then_inc(mask_done, 1)

            def place_v(v, g):
                if not active(v):
                    return
                pool.wait_ge(taken["vproj"], due(pool, v + 1))
                pool.wait_ge(pv_full, due(pool, (v - 1) * 4 + (g + 1)))
                copy(v_aug[:, :, GH * g:GH * (g + 1), 0:DH], v_nat[:, :, GH * g:GH * (g + 1), :]).then_inc(v_copied, 1)

            def inv_std(v, which):
                if not active(v):
                    return
                pool.wait_ge(ln_done[which], due(pool, v))
                pool.wait_ge(ln_mv[which], due(pool, v + 1))
                pool.tensor_tensor(ve[which][:, :], mv[which][:, :, 1], eps_t[:, :], ALU.add).then_inc(ln_ve[which], 1)
                pool.wait_ge(ln_ve[which], due(pool, v + 1))
                pool.tensor_tensor(rstd[which][:, :], ve[which][:, :], mhalf[:, :], ALU.pow).then_inc(ln_rstd[which], 1)

            def table(v, k):
                layer = layer_of(v)
                return rope[:, bass.ds(layer * (4 * SEQ) + k * 2 * SEQ, 2 * SEQ)]

            def rotate(v, step):
                if not active(v):
                    return
                if step == 0:
                    pool.wait_ge(part2, due(pool, v))
                    pool.wait_ge(part0, due(pool, v))
                    pool.wait_ge(taken["qproj"], due(pool, v + 1))
                    pool.wait_ge(taken["kproj"], due(pool, v + 1))
                    pool.tensor_tensor(qk_rot[:, :], qk[:, :], table(v, 0), ALU.mult).then_inc(rope_c, 1)
                elif step == 1:
                    pool.wait_ge(swap_in, due(pool, (v + 1) * 32))
                    pool.tensor_tensor(qk_rest[:, :], qk_sw[:, :], table(v, 1), ALU.mult).then_inc(rope_s, 1)
                else:
                    pool.wait_ge(rope_c, due(pool, v + 1))
                    pool.wait_ge(rope_s, due(pool, v + 1))
                    pool.tensor_tensor(qk_rot[:, :], qk_rot[:, :], qk_rest[:, :], ALU.add).then_inc(rope_done, 1)

            def rest(v, k):
                if not active(v):
                    return
                p = parts[:, k, :, :].rearrange("p a n -> p (a n)")
                if k == 0:
                    pool.wait_ge(rope_done, due(pool, v + 1))
                    pool.wait_ge(part0, due(pool, v + 1))
                    pool.tensor_tensor(qk_rest[:, :], qk_rot[:, :], p, ALU.subtract).then_inc(rest0, 1)
                else:
                    pool.wait_ge(rest0, due(pool, v + 1))
                    pool.wait_ge(part1, due(pool, v + 1))
                    pool.tensor_tensor(parts[:, 2, :, :].rearrange("p a n -> p (a n)"), qk_rest[:, :], p,
                                       ALU.subtract).then_inc(part2, 1)

            def shift_diff(v):
                if not active(v):
                    return
                pool.wait_ge(f_xk_done, due(pool, v))
                pool.wait_ge(f_xr_done, due(pool, v))
                pool.wait_ge(taken["fx_t"], due(pool, v + 1))
                pool.tensor_tensor(fd[:, :], fx[:, 1:1 + SEQ], fx[:, 0:SEQ], ALU.subtract).then_inc(f_diff, 1)

            def square(v):
                if not active(v):
                    return
                pool.wait_ge(made["fv"], due(pool, v))
                pool.wait_ge(taken["fk"], due(pool, v + 1))
                pool.tensor_tensor(k_sq[:, :], k_relu[:, :], k_relu[:, :], ALU.mult).then_inc(sq_done, 1)

            def body(u):
                for s in range(SLOTS):
                    for i in range(P1_UNITS):
                        if i == 0:
                            split_max(*max_group(u, s))
                        if i == 1:
                            place_v(u, s)
                        if i in (3, 7, 9, 10):
                            mask(*pass2_group(u, s), (3, 7, 9, 10).index(i))
                        if s == 0:
                            if i == 2:
                                inv_std(u + 1, 0)
                            if i == 8:
                                inv_std(u - 2, 1)
                        if s == 1:
                            if i == 6:
                                rotate(u + 1, 0)
                            if i == 9:
                                shift_diff(u - 2)
                        if s == 2:
                            if i == 2:
                                rotate(u + 1, 1)
                            if i == 4:
                                rotate(u + 1, 2)
                            if i == 8:
                                square(u - 2)
                            if i == 10:
                                rest(u + 1, 0)
                        if s == 3:
                            if i == 4:
                                rest(u + 1, 1)

            run(pool, body)


def kernel(**inputs):
    import numpy as np
    import concourse.bacc as bacc
    from concourse.bass_utils import run_bass_kernel_spmd

    a = {k: np.asarray(v) for k, v in inputs.items()}

    def cols(*mats):
        return np.ascontiguousarray(np.concatenate(mats, axis=1))

    def per_head(w):
        return w.reshape(DM, DM).T

    d_of = np.array([0, 2, 4, 6, 1, 3, 5, 7])
    order = np.array([(2 * pair + par) * DH + d for d in d_of for par in range(2) for pair in range(HEADS // 2)])
    w = cols(per_head(a["L0_attn_a_WQ"])[:, order], per_head(a["L0_attn_a_WK"])[:, order], per_head(a["L0_attn_a_WV"]),
             a["L0_attn_a_WO"].transpose(0, 2, 1).reshape(DM, DM),
             a["L0_attn_b_W_q"].T[:, order], a["L0_attn_b_W_k"].T[:, order], a["L0_attn_b_W_v"].T, a["L0_attn_b_W_o"].T)
    wf = cols(a["L0_ffn_W_r"].T, a["L0_ffn_W_k"].T, a["L0_ffn_W_v"].T)
    mu = np.ascontiguousarray(np.stack([a["L0_ffn_mu_r"], a["L0_ffn_mu_k"]], axis=1))

    inv_freq = (1.0 / 10000.0 ** (np.arange(0, DH, 2, dtype=np.float32) / np.float32(DH))).astype(np.float32)
    angle = (np.arange(SEQ, dtype=np.float32)[:, None] * inv_freq[None, :]).astype(np.float32)
    d = d_of[np.arange(P) // HEADS]
    cos = np.cos(angle.astype(np.float64)).T[d // 2]
    sin = np.sin(angle.astype(np.float64)).T[d // 2] * np.where(d % 2 == 0, -1.0, 1.0)[:, None]
    tables = []
    for c, s, scale in ((np.ones_like(cos), np.zeros_like(sin), DH ** -0.5), (cos, sin, DM ** -0.5)):
        tables += [c * scale, c, s * scale, s]
    rope = np.concatenate(tables, axis=1).astype(np.float32)

    arrays = {"x": np.ascontiguousarray(a["L0_attn_a_x"]), "w": w, "wf": wf, "mu": mu, "rope": rope}
    nc = bacc.Bacc("TRN2", target_bir_lowering=False, num_devices=1)
    args = [nc.dram_tensor(f"in_{n}", arr.shape, mybir.dt.from_np(arr.dtype), kind="ExternalInput").ap()
            for n, arr in arrays.items()]
    out = nc.dram_tensor("out", (BATCH, SEQ, DM), F32, kind="ExternalOutput").ap()
    build(nc, *args, out)
    r = run_bass_kernel_spmd(nc, [{f"in_{n}": arr for n, arr in arrays.items()}], core_ids=[0])
    return r.results[0]["out"]
```

```python
from contextlib import ExitStack

import concourse.bass as bass
from concourse import mybir

F32 = mybir.dt.float32
BF16 = mybir.dt.bfloat16
ALU = mybir.AluOpType
ACT = mybir.ActivationFunctionType
AX = mybir.AxisListType

P = 128
BATCH, SEQ, DM = 8, 512, 128
HEADS, DH = 16, 8
LAYERS = 2
UNITS = LAYERS * BATCH
TILES = SEQ // P
GROUPS, GH = 4, 4
SLOTS = GROUPS
PARTS = 3
Q_TERMS = [0, 0, 0, 1, 1, 2]
K_TERMS = [0, 1, 2, 0, 1, 0]
TERM_RUNS = [(0, 0, 3, 0, 0), (0, 3, 2, 1, 0), (0, 5, 1, 2, 0), (1, 0, 3, 0, 1), (1, 3, 2, 0, 1), (1, 5, 1, 0, 0)]
TERM_ROWS = DH * len(Q_TERMS)
AUG_ROWS = TERM_ROWS + PARTS
HALF = 64
OW = 32
EPS = 1e-5
MASKED = -3.0e38

P1_UNITS = 12
P2_UNITS = 12
RING = 3
P1_LIST = [(0, [0, 2]), (0, [1, 3]), (1, [0, 2]), (1, [1, 3])] + [(2, [j]) for j in range(4)] + [(3, [j]) for j in range(4)]
P2_LIST = [(0, [j]) for j in range(4)] + [(1, [j]) for j in range(4)] + [(2, [0, 2]), (2, [1, 3]), (3, [0, 2]), (3, [1, 3])]
P2_UP_TO = [4, 8, 10, 12]
P_OFF = [0, 512, 896, 1152]
P_LEN = 1280

STEPS = P1_UNITS
PV_AT = {1: 0, 3: 1, 6: 2, 8: 3}
MASK_AT = {3: 0, 7: 1, 9: 2, 11: 3}
ROUNDS = [
    [(0, "xn_t", 1, 0), (2, "qproj", 1, 0), (4, "max_t", -1, 3), (6, "kproj", 1, 0), (8, "attn_t", -2, 0),
     (10, "oproj", -2, 0)],
    [(4, "max_t", 0, 0), (9, "fx_t", -2, 0)],
    [(2, "fk", -2, 0), (4, "max_t", 0, 1), (6, "fr", -2, 0), (9, "fv", -2, 0)],
    [(1, "onat", -1, 0), (3, "max_t", 0, 2), (5, "onat", -1, 1), (7, "onat", -1, 2), (9, "onat", -1, 3),
     (11, "vproj", 1, 0)],
]
PER_UNIT = {"attn_t": 1, "max_t": 4, "oproj": 1, "xn_t": 1, "qproj": 1, "kproj": 1, "fx_t": 1, "fk": 1,
            "fr": 1, "onat": 4, "fv": 1, "vproj": 1}
FIRST_BODY, LOOP_FROM, LOOP_TO, LAST_BODY = -2, 3, UNITS - 2, UNITS + 1


def active(v):
    return not isinstance(v, int) or 0 <= v < UNITS


def layer_of(v):
    return v // BATCH if isinstance(v, int) else (v >> 3).with_bounds(min_val=0, max_val=LAYERS - 1)


def max_group(u, s):
    return (u, s - 1) if s >= 1 else (u - 1, 3)


def pass2_group(u, s):
    return (u, s - 2) if s >= 2 else (u - 1, s + 2)


def pv_group(u, s):
    return (u, 0) if s == 3 else (u - 1, s + 1)


def build(nc, x_d, w_d, wf_d, mu_d, rope_d, out_d):
    with ExitStack() as ctx:
        def sb(name, shape, dt=F32):
            return ctx.enter_context(nc.sbuf_tensor(name, shape, dt))

        def ps(name, shape):
            return ctx.enter_context(nc.psum_tensor(name, shape, F32))

        def sem(name):
            return ctx.enter_context(nc.semaphore(name))

        x_sb = sb("x_sb", [P, UNITS * SEQ])
        w_all = sb("w_all", [P, LAYERS * 4 * DM])
        w_qkv = sb("w_qkv", [P, 3 * DM])
        w_o = sb("w_o", [P, DM])
        w_ffn = sb("w_ffn", [P, 3 * DM])
        mu = sb("mu", [P, 2])
        rope = sb("rope", [P, LAYERS * 2 * 2 * SEQ])
        ident = sb("ident", [P, P])
        ident_b = sb("ident_b", [P, P], BF16)
        causal = sb("causal", [P, GH * P], BF16)
        eps_t = sb("eps_t", [P, TILES])
        mhalf = sb("mhalf", [P, TILES])
        zero_t = sb("zero_t", [P, TILES])
        bn = [sb(f"bn{i}", [P, TILES, 6]) for i in range(2)]
        mv = [sb(f"mv{i}", [P, TILES, 2]) for i in range(2)]
        ve = [sb(f"ve{i}", [P, TILES]) for i in range(2)]
        rstd = [sb(f"rstd{i}", [P, TILES]) for i in range(2)]
        nmean = [sb(f"nmean{i}", [P, TILES]) for i in range(2)]
        nbias = [sb(f"nbias{i}", [P, TILES]) for i in range(2)]
        xn = [sb(f"xn{i}", [P, SEQ]) for i in range(2)]
        xn_t = sb("xn_t", [P, SEQ])
        qk = sb("qk", [P, 2 * SEQ])
        qk_sw = sb("qk_sw", [P, 2 * SEQ])
        qk_rot = sb("qk_rot", [P, 2 * SEQ])
        qk_rest = sb("qk_rest", [P, 2 * SEQ])
        parts = sb("parts", [P, PARTS, 2, SEQ], BF16)
        aug = sb("aug", [P, 2, HEADS // 2, SEQ], BF16)
        v_nat = sb("v_nat", [P, TILES, HEADS, DH])
        v_aug = sb("v_aug", [P, TILES, HEADS, OW])
        nmax = [sb(f"nmax{i}", [P, TILES, 2, 2]) for i in range(2)]
        nmax_r = sb("nmax_r", [P, TILES, 2, 2])
        nmax_p = sb("nmax_p", [P, TILES, 2, 2, PARTS], BF16)
        nmax_t = sb("nmax_t", [2 * PARTS * 2, SEQ], BF16)
        probs = [sb(f"probs{i}", [P, GH, P_LEN]) for i in range(2)]
        o_t = sb("o_t", [P, GROUPS, SEQ])
        rsum = sb("rsum", [P, TILES, HEADS])
        attn = sb("attn", [P, TILES, HEADS, DH])
        attn_t = sb("attn_t", [P, SEQ])
        x_mid = sb("x_mid", [P, SEQ])
        fx = sb("fx", [P, 1 + SEQ])
        fd = sb("fd", [P, SEQ])
        f_xk = sb("f_xk", [P, SEQ])
        f_xr = sb("f_xr", [P, SEQ])
        k_relu = sb("k_relu", [P, SEQ])
        k_sq = sb("k_sq", [P, SEQ])
        gate = sb("gate", [P, SEQ])
        gate1 = sb("gate1", [P, SEQ])
        gated = sb("gated", [P, SEQ])

        terms_d = nc.dram_tensor("terms", (2, len(Q_TERMS), P, SEQ), BF16).ap()

        p1 = ps("p1", [P, RING, 512])
        p2 = ps("p2", [P, RING, 512])
        pv = ps("pv", [P, 512])
        shared = ps("shared", [P, 512])
        shared_b = shared[:, :].bitcast(BF16)

        x_in = [sem(f"x_in{i}") for i in range(3)]
        const_in = sem("const_in")
        setup = sem("setup")
        zeroed = sem("zeroed")
        x_ready = sem("x_ready")
        w_in, wo_in, swap_in = sem("w_in"), sem("wo_in"), sem("swap_in")
        aug_in = [sem(f"aug_in{g}") for g in range(GROUPS)]
        terms_out = sem("terms_out")
        max_in = [sem(f"max_in{g}") for g in range(GROUPS)]
        made = {n: sem(f"made_{n}") for n in PER_UNIT}
        taken = {n: sem(f"taken_{n}") for n in PER_UNIT}
        ln_stat = [sem(f"ln_stat{i}") for i in range(2)]
        ln_mv = [sem(f"ln_mv{i}") for i in range(2)]
        ln_ve = [sem(f"ln_ve{i}") for i in range(2)]
        ln_rstd = [sem(f"ln_rstd{i}") for i in range(2)]
        ln_nmean = [sem(f"ln_nmean{i}") for i in range(2)]
        ln_bias = [sem(f"ln_bias{i}") for i in range(2)]
        ln_done = [sem(f"ln_done{i}") for i in range(2)]
        rope_c, rope_s, rope_done = sem("rope_c"), sem("rope_s"), sem("rope_done")
        part0, rest0, part1, part2 = sem("part0"), sem("rest0"), sem("part1"), sem("part2")
        v_copied = sem("v_copied")
        p1_full, p1_max = sem("p1_full"), sem("p1_max")
        max_p = sem("max_p")
        p2_full, exp_done, mask_done = sem("p2_full"), sem("exp_done"), sem("mask_done")
        pv_full, o_out = sem("pv_full"), sem("o_out")
        rsum_done = sem("rsum_done")
        f_diff, f_xk_done, f_xr_done, sq_done = sem("f_diff"), sem("f_xk_done"), sem("f_xr_done"), sem("sq_done")
        gate_done, gated_done = sem("gate_done"), sem("gated_done")
        out_done = sem("out_done")
        SETUP = 11

        block = ctx.enter_context(nc.Block())

        def due(eng, count):
            if isinstance(count, int):
                return max(count, 0)
            value = eng.snap(eng.to_reg(count))
            eng.wait_ge(setup, SETUP)
            return value

        def x_at(v):
            if isinstance(v, int):
                return x_sb[:, (v % UNITS) * SEQ:(v % UNITS + 1) * SEQ]
            return x_sb[:, bass.ds((v % UNITS) * SEQ, SEQ)]

        def rope_table(v, k, side=None):
            first, n = (0, 2 * SEQ) if side is None else (side * SEQ, SEQ)
            return rope[:, bass.ds(layer_of(v) * (4 * SEQ) + (k * 2 * SEQ + first), n)]

        def bank_before(u, s, step):
            order = [(ss, st, n, du, k) for ss in range(SLOTS) for st, n, du, k in ROUNDS[ss]]
            at = [(ss, st) for ss, st, *_ in order].index((s, step))
            for back in range(1, 3 * len(order)):
                i = at - back
                body = i // len(order)
                _, _, n, du, k = order[i % len(order)]
                v = u + (body + du)
                if isinstance(v, int) and v < 0 and u + body < FIRST_BODY:
                    return None
                if active(v):
                    return taken[n], v * PER_UNIT[n] + (k + 1)
            return None

        def run(eng, body):
            for u in range(FIRST_BODY, LOOP_FROM):
                body(u)
            with eng.Fori(LOOP_FROM, LOOP_TO) as u:
                body(u)
            for u in range(LOOP_TO, LAST_BODY + 1):
                body(u)

        @block.sync
        def _(sp):
            sp.dma_start(w_all[:, :], w_d).then_inc(const_in, 16)
            xr = x_d.rearrange("b (t p) d -> b p t d", p=P)

            def load_x(b, s):
                sp.dma_start(x_sb[:, b * SEQ:(b + 1) * SEQ].rearrange("p (t d) -> p t d", d=DM), xr[b]).then_inc(s, 16)

            load_x(0, x_in[0])
            load_x(1, x_in[1])
            sp.dma_start(rope[:, :], rope_d).then_inc(const_in, 16)
            sp.dma_start(w_ffn[:, :], wf_d).then_inc(const_in, 16)
            sp.dma_start(mu[:, :], mu_d).then_inc(const_in, 16)
            sp.wait_ge(const_in, 64)
            for b in range(2, BATCH):
                load_x(b, x_in[2])
            sp.wait_ge(setup, SETUP)

            def load_w(v):
                if not active(v):
                    return
                sp.wait_ge(made["vproj"], due(sp, v))
                layer = layer_of(v)
                sp.dma_start(w_qkv[:, :], w_all[:, bass.ds(layer * (4 * DM), 3 * DM)]).then_inc(w_in, 16)

            def load_wo(v):
                if not active(v):
                    return
                sp.wait_ge(made["oproj"], due(sp, v))
                layer = layer_of(v)
                sp.dma_start(w_o[:, :], w_all[:, bass.ds(layer * (4 * DM) + 3 * DM, DM)]).then_inc(wo_in, 16)

            def swap(v):
                if not active(v):
                    return
                sp.wait_ge(taken["qproj"], due(sp, v + 1))
                sp.wait_ge(taken["kproj"], due(sp, v + 1))
                sp.wait_ge(rope_s, due(sp, v))
                for k in range(2):
                    a, b = slice(k * HALF, (k + 1) * HALF), slice((1 - k) * HALF, (2 - k) * HALF)
                    sp.dma_start(qk_sw[a, :], qk[b, :]).then_inc(swap_in, 16)

            def send_terms(v):
                if not active(v):
                    return
                sp.wait_ge(part0, due(sp, (v + 1) * 2))
                sp.wait_ge(part1, due(sp, (v + 1) * 2))
                sp.wait_ge(part2, due(sp, v + 1))
                for g in range(GROUPS):
                    sp.wait_ge(aug_in[g], due(sp, v * 32))
                for side, t0, n, part, step in TERM_RUNS:
                    src = parts[:, part, side, :].unsqueeze(1).broadcast_to([P, n, SEQ]) if step == 0 \
                        else parts[:, part:part + n, side, :]
                    sp.dma_start(terms_d[side, t0:t0 + n].rearrange("t p n -> p t n"), src).then_inc(terms_out, 16)

            def fetch_terms(v, g):
                if not active(v):
                    return
                sp.wait_ge(terms_out, due(sp, (v + 1) * (16 * len(TERM_RUNS))))
                sp.wait_ge(p2_full, due(sp, (v - 1) * (P2_UNITS * GROUPS) + P2_UNITS * (g + 1)))
                src = terms_d.rearrange("s t (d par pair) n -> par (t d) s pair n", par=2, d=DH)
                for par in range(2):
                    sp.dma_start(aug[HALF * par:HALF * par + TERM_ROWS, :, 2 * g:2 * g + 2, :],
                                 src[par][:, :, 2 * g:2 * g + 2, :]).then_inc(aug_in[g], 16)

            def put_max(v, g):
                if not active(v):
                    return
                sp.wait_ge(taken["max_t"], due(sp, v * 4 + (g + 1)))
                for par in range(2):
                    row = HALF * par + TERM_ROWS
                    for jj in range(2):
                        src = nmax_t[6 * par + 3 * jj:6 * par + 3 * jj + PARTS, :]
                        sp.dma_start(aug[row:row + PARTS, 0, 2 * g + jj, :], src).then_inc(max_in[g], 16)

            def body(u):
                fetch_terms(u, 1)
                put_max(u - 1, 3)
                swap(u + 1)
                fetch_terms(u, 2)
                put_max(u, 0)
                load_wo(u - 1)
                fetch_terms(u, 3)
                put_max(u, 1)
                send_terms(u + 1)
                put_max(u, 2)
                fetch_terms(u + 1, 0)
                load_w(u + 2)

            run(sp, body)
            orr = out_d.rearrange("b (t p) d -> b p t d", p=P)
            for b in range(BATCH):
                sp.wait_ge(x_ready, 2 * BATCH + b + 1)
                sp.dma_start(orr[b], x_sb[:, b * SEQ:(b + 1) * SEQ].rearrange("p (t d) -> p t d", d=DM)).then_inc(out_done, 16)
            sp.wait_ge(out_done, 16 * BATCH)

        @block.tensor
        def _(pe):
            pe.wait_ge(setup, SETUP)
            pe.wait_ge(const_in, 64)

            def pass1(u, g, i):
                if not active(u):
                    return
                if i == 0:
                    pe.wait_ge(aug_in[g], due(pe, (u + 1) * 32))
                n = GROUPS * P1_UNITS
                pe.wait_ge(p1_max, due(pe, u * n + (P1_UNITS * g + i - RING + 1)))
                bank = i % RING
                qt, heads = P1_LIST[i]
                length = (qt + 1) * P
                out = p1[:, bank, 0:len(heads) * length].rearrange("p (h k) -> p h k", h=len(heads))
                pe.matmul(out[:, :, qt * P:length], ident_b[:, :],
                          causal[:, 0:len(heads) * P].rearrange("p (h k) -> p h k", h=len(heads)),
                          start=True, stop=False, skip_group_check=True)
                for n_, j in enumerate(heads):
                    row, pair = HALF * (j % 2), 2 * g + j // 2
                    last = pe.matmul(out[:, n_, :], aug[row:row + TERM_ROWS, 0, pair, qt * P:(qt + 1) * P],
                                     aug[row:row + TERM_ROWS, 1, pair, 0:length],
                                     start=False, stop=True, skip_group_check=True)
                last.then_inc(p1_full, 1)

            def pass2(v, g, i):
                if not active(v):
                    return
                if i == 0:
                    pe.wait_ge(max_in[g], due(pe, (v + 1) * (16 * 4)))
                n = GROUPS * P2_UNITS
                pe.wait_ge(exp_done, due(pe, v * n + (P2_UNITS * g + i - RING + 1)))
                kt, heads = P2_LIST[i]
                width = SEQ - kt * P
                for m, j in enumerate(heads):
                    row, pair = HALF * (j % 2), 2 * g + j // 2
                    last = pe.matmul(p2[:, i % RING, m * width:(m + 1) * width],
                                     aug[row:row + AUG_ROWS, 1, pair, kt * P:(kt + 1) * P],
                                     aug[row:row + AUG_ROWS, 0, pair, kt * P:SEQ], start=True, stop=True)
                last.then_inc(p2_full, 1)

            def times_v(v, g, kt):
                if not active(v):
                    return
                if kt == 0:
                    pe.wait_ge(v_copied, due(pe, v * 4 + (g + 1)))
                    pe.wait_ge(o_out, due(pe, v * 4 + g))
                pe.wait_ge(mask_done, due(pe, v * 16 + (4 * g + kt + 1)))
                for j in range(GH):
                    last = pe.matmul(pv[OW * j:OW * (j + 1), kt * P:SEQ], v_aug[:, kt, GH * g + j, :],
                                     probs[g % 2][:, j, P_OFF[kt]:P_OFF[kt] + SEQ - kt * P],
                                     start=(kt == 0), stop=(kt == TILES - 1), tile_position=(0, OW * j))
                if kt == TILES - 1:
                    last.then_inc(pv_full, 1)

            def tile_t(i):
                return slice(i * P, (i + 1) * P)

            def shared_round(u, s, step, name, dv, k):
                v = u + dv
                if not active(v):
                    return
                before = bank_before(u, s, step)
                if before:
                    pe.wait_ge(before[0], due(pe, before[1]))
                if name == "xn_t":
                    pe.wait_ge(ln_done[0], due(pe, (v + 1) * TILES))
                    for t in range(TILES):
                        last = pe.transpose(shared[:, tile_t(t)], xn[0][:, tile_t(t)], ident[:, :])
                elif name in ("qproj", "kproj"):
                    pe.wait_ge(taken["xn_t"], due(pe, v + 1))
                    pe.wait_ge(w_in, due(pe, (v + 1) * 16))
                    w = 0 if name == "qproj" else 1
                    last = pe.matmul(shared[:, :], w_qkv[:, tile_t(w)], xn_t[:, :], start=True, stop=True)
                elif name == "vproj":
                    for t in range(TILES):
                        last = pe.matmul(shared[:, tile_t(t)], xn_t[:, tile_t(t)], w_qkv[:, tile_t(2)], start=True, stop=True)
                elif name == "max_t":
                    pe.wait_ge(max_p, due(pe, v * 16 + (4 * k + 4)))
                    for t in range(TILES):
                        last = pe.transpose(shared_b[0:4 * PARTS, tile_t(t)],
                                            nmax_p[:, t, :, :, :].rearrange("p a b k -> p (a b k)"), ident_b[:, :])
                elif name == "onat":
                    pe.wait_ge(o_out, due(pe, v * 4 + 4))
                    for g in range(GROUPS):
                        last = pe.transpose(shared[:, tile_t(g)], o_t[:, g, tile_t(k)], ident[:, :])
                elif name == "attn_t":
                    for t in range(TILES):
                        last = pe.transpose(shared[:, tile_t(t)], attn[:, t, :, :].rearrange("p h d -> p (h d)"), ident[:, :])
                elif name == "oproj":
                    pe.wait_ge(taken["attn_t"], due(pe, v + 1))
                    pe.wait_ge(wo_in, due(pe, (v + 1) * 16))
                    for t in range(TILES):
                        last = pe.matmul(shared[:, tile_t(t)], attn_t[:, tile_t(t)], w_o[:, :], start=True, stop=True)
                elif name == "fx_t":
                    pe.wait_ge(ln_done[1], due(pe, (v + 1) * TILES))
                    for t in range(TILES):
                        last = pe.transpose(shared[:, tile_t(t)], xn[1][:, tile_t(t)], ident[:, :])
                elif name == "fk":
                    pe.wait_ge(f_xk_done, due(pe, v + 1))
                    last = pe.matmul(shared[:, :], w_ffn[:, tile_t(1)], f_xk[:, :], start=True, stop=True)
                elif name == "fr":
                    pe.wait_ge(f_xr_done, due(pe, v + 1))
                    for t in range(TILES):
                        last = pe.matmul(shared[:, tile_t(t)], f_xr[:, tile_t(t)], w_ffn[:, tile_t(0)], start=True, stop=True)
                elif name == "fv":
                    pe.wait_ge(sq_done, due(pe, v + 1))
                    for t in range(TILES):
                        last = pe.matmul(shared[:, tile_t(t)], k_sq[:, tile_t(t)], w_ffn[:, tile_t(2)], start=True, stop=True)
                last.then_inc(made[name], 1)

            def body(u):
                for s in range(SLOTS):
                    for i in range(STEPS):
                        pass1(u, s, i)
                        pass2(*pass2_group(u, s), i)
                        if i in PV_AT:
                            times_v(*pv_group(u, s), PV_AT[i])
                        for step, name, dv, k in ROUNDS[s]:
                            if step == i:
                                shared_round(u, s, step, name, dv, k)

            run(pe, body)

        @block.scalar
        def _(act):
            act.wait_ge(setup, SETUP)

            def exps(v, g, i):
                if not active(v):
                    return
                if i == 0:
                    act.wait_ge(pv_full, due(act, v * 4 + (g - 1)))
                act.wait_ge(p2_full, due(act, v * (GROUPS * P2_UNITS) + (P2_UNITS * g + i + 1)))
                kt, heads = P2_LIST[i]
                width = SEQ - kt * P
                src = p2[:, i % RING, 0:len(heads) * width].rearrange("p (h q) -> p h q", h=len(heads))
                dst = probs[g % 2][:, heads[0]:heads[-1] + 1:2, P_OFF[kt]:P_OFF[kt] + width]
                act.activation(dst, src, ACT.Exp).then_inc(exp_done, 1)

            def out_copy(v, g):
                if not active(v):
                    return
                act.wait_ge(made["onat"], due(act, v * 4))
                act.wait_ge(pv_full, due(act, v * 4 + (g + 1)))
                act.copy(o_t[:, g, :], pv[:, :]).then_inc(o_out, 1)

            def take(v, name, k):
                if not active(v) or name in ("onat", "oproj", "fv"):
                    return
                if name == "xn_t":
                    act.wait_ge(made["vproj"], due(act, v))
                    act.wait_ge(made["xn_t"], due(act, v + 1))
                    act.copy(xn_t[:, :], shared[:, :]).then_inc(taken[name], 1)
                elif name in ("qproj", "kproj"):
                    side = 0 if name == "qproj" else 1
                    act.wait_ge(swap_in, due(act, v * 32))
                    act.wait_ge(rope_c, due(act, v * 2))
                    act.wait_ge(made[name], due(act, v + 1))
                    act.copy(qk[:, side * SEQ:(side + 1) * SEQ], shared[:, :]).then_inc(taken[name], 1)
                elif name == "vproj":
                    act.wait_ge(v_copied, due(act, v * 4))
                    act.wait_ge(made[name], due(act, v + 1))
                    act.copy(v_nat[:, :, :, :].rearrange("p t h d -> p (t h d)"), shared[:, :]).then_inc(taken[name], 1)
                elif name == "max_t":
                    w, k0 = (v, k - 1) if k else (v - 1, 3)
                    if active(w):
                        act.wait_ge(max_in[k0], due(act, (w + 1) * (16 * 4)))
                    act.wait_ge(made[name], due(act, v * 4 + (k + 1)))
                    act.copy(nmax_t[:, :], shared_b[0:4 * PARTS, 0:SEQ]).then_inc(taken[name], 1)
                elif name == "attn_t":
                    act.wait_ge(made["oproj"], due(act, v))
                    act.wait_ge(made[name], due(act, v + 1))
                    act.copy(attn_t[:, :], shared[:, :]).then_inc(taken[name], 1)
                elif name == "fx_t":
                    act.wait_ge(f_xk_done, due(act, v))
                    act.wait_ge(f_xr_done, due(act, v))
                    act.wait_ge(made[name], due(act, v + 1))
                    act.copy(fx[:, 1:1 + SEQ], shared[:, :]).then_inc(taken[name], 1)
                elif name == "fk":
                    act.wait_ge(sq_done, due(act, v))
                    act.wait_ge(made[name], due(act, v + 1))
                    act.activation(k_relu[:, :], shared[:, :], ACT.Relu).then_inc(taken[name], 1)
                elif name == "fr":
                    act.wait_ge(gate_done, due(act, v))
                    act.wait_ge(made[name], due(act, v + 1))
                    act.activation(gate[:, :], shared[:, :], ACT.Tanh, scale=0.5).then_inc(taken[name], 1)

            def normalise(v, which, x, t):
                if not active(v):
                    return
                if t == 0:
                    act.wait_ge(ln_rstd[which], due(act, v + 1))
                    act.wait_ge(ln_bias[which], due(act, v + 1))
                    act.wait_ge(made["xn_t" if which == 0 else "fx_t"], due(act, v))
                act.activation(xn[which][:, t * P:(t + 1) * P], x[:, t * P:(t + 1) * P], ACT.Identity,
                               scale=rstd[which][:, t:t + 1], bias=nbias[which][:, t:t + 1]).then_inc(ln_done[which], 1)

            def cast_part(v, k, side):
                if not active(v):
                    return
                half = slice(side * SEQ, (side + 1) * SEQ)
                if k == 0:
                    act.wait_ge(terms_out, due(act, v * (16 * len(TERM_RUNS))))
                    act.wait_ge(rope_done, due(act, v + 1))
                    act.copy(parts[:, 0, side, :], qk_rot[:, half]).then_inc(part0, 1)
                else:
                    act.wait_ge(rest0, due(act, v + 1))
                    act.copy(parts[:, 1, side, :], qk_rest[:, half]).then_inc(part1, 1)

            def body(u):
                for s in range(SLOTS):
                    for i in range(STEPS):
                        exps(*pass2_group(u, s), i)
                        for step, name, dv, k in ROUNDS[s]:
                            if step == i:
                                take(u + dv, name, k)
                        if i == 9:
                            out_copy(*pv_group(u, s))
                        if s == 1 and 3 <= i < 3 + TILES:
                            normalise(u - 2, 1, x_mid, i - 3)
                        if s == 1 and i in (10, 11):
                            cast_part(u + 1, 0, i - 10)
                        if s == 2 and i in (6, 7):
                            cast_part(u + 1, 1, i - 6)
                        if s == 3 and 7 <= i < 7 + TILES and active(u + 2):
                            normalise(u + 2, 0, x_at(u + 2), i - 7)

            run(act, body)

        @block.vector
        def _(dve):
            dve.memset(fx[:, 0:1], 0.0).then_inc(setup, 1)
            dve.memset(eps_t[:, :], EPS).then_inc(setup, 1)
            dve.memset(mhalf[:, :], -0.5).then_inc(setup, 1)
            dve.memset(zero_t[:, :], 0.0).then_inc(setup, 1)
            for par in range(2):
                ones = slice(HALF * par + HALF // 2, HALF * (par + 1))
                dve.memset(aug[ones, 1, :, :], 1.0).then_inc(setup, 1)
            dve.wait_ge(x_in[0], 16)
            dve.sem_inc(x_ready, BATCH)
            dve.wait_ge(setup, SETUP)

            def row_max(u, g, i):
                if not active(u):
                    return
                if i == 0:
                    w, g0 = (u, g - 2) if g >= 2 else (u - 1, g + 2)
                    if active(w):
                        dve.wait_ge(max_p, due(dve, w * 16 + (4 * g0 + 3)))
                dve.wait_ge(p1_full, due(dve, u * (GROUPS * P1_UNITS) + (P1_UNITS * g + i + 1)))
                qt, heads = P1_LIST[i]
                length = (qt + 1) * P
                src = p1[:, i % RING, 0:len(heads) * length].rearrange("p (h k) -> p h k", h=len(heads))
                jj, par = heads[0] // 2, heads[0] % 2
                if len(heads) == 2:
                    dst = nmax[g % 2][:, qt, par, :]
                else:
                    dst = nmax[g % 2][:, qt, par, jj:jj + 1]
                dve.tensor_reduce(dst, src, AX.X, ALU.max, negate=True).then_inc(p1_max, 1)

            def stats(v, which, x):
                if not active(v):
                    return
                dve.wait_ge(ln_bias[which], due(dve, v))
                for t in range(TILES):
                    last = dve.bn_stats(bn[which][:, t, :], x[:, t * P:(t + 1) * P])
                last.then_inc(ln_stat[which], 1)
                dve.wait_ge(ln_stat[which], due(dve, v + 1))
                for t in range(TILES):
                    last = dve.bn_aggr(mv[which][:, t, :], bn[which][:, t, :])
                last.then_inc(ln_mv[which], 1)

            def first_stats(v):
                if not active(v):
                    return
                if isinstance(v, int) and v < 3:
                    dve.wait_ge(x_in[v], 16 if v < 2 else 16 * (BATCH - 2))
                dve.wait_ge(x_ready, due(dve, v + 1))
                stats(v, 0, x_at(v))

            def divide(v, k):
                if not active(v):
                    return
                if k == 0:
                    dve.wait_ge(made["attn_t"], due(dve, v))
                dve.wait_ge(made["onat"], due(dve, v * 4 + (k + 1)))
                o = shared[:, :].rearrange("p (h c) -> p h c", c=OW)
                dve.reciprocal(rsum[:, k, :], o[:, :, DH]).then_inc(rsum_done, 1)
                dve.wait_ge(rsum_done, due(dve, v * 4 + (k + 1)))
                dve.tensor_tensor(attn[:, k, :, :], o[:, :, 0:DH],
                                  rsum[:, k, :].unsqueeze(2).broadcast_to([P, HEADS, DH]), ALU.mult)\
                    .then_inc(taken["onat"], 1)

            def add_attn(v):
                if not active(v):
                    return
                dve.wait_ge(made["oproj"], due(dve, v + 1))
                dve.wait_ge(x_ready, due(dve, v + BATCH))
                dve.tensor_tensor(x_mid[:, :], shared[:, :], x_at(v), ALU.add).then_inc(taken["oproj"], 1)

            def rotate_cos(v, side):
                if not active(v):
                    return
                half = slice(side * SEQ, (side + 1) * SEQ)
                dve.wait_ge(part0, due(dve, v * 2))
                dve.wait_ge(rest0, due(dve, v))
                dve.wait_ge(taken["kproj" if side else "qproj"], due(dve, v + 1))
                dve.tensor_tensor(qk_rot[:, half], qk[:, half], rope_table(v, 0, side), ALU.mult).then_inc(rope_c, 1)

            def shift_diff(v):
                if not active(v):
                    return
                dve.wait_ge(f_xk_done, due(dve, v))
                dve.wait_ge(f_xr_done, due(dve, v))
                dve.wait_ge(taken["fx_t"], due(dve, v + 1))
                dve.tensor_tensor(fd[:, :], fx[:, 1:1 + SEQ], fx[:, 0:SEQ], ALU.subtract).then_inc(f_diff, 1)

            def mix(v, k):
                if not active(v):
                    return
                dst, done, reader = ((f_xr, f_xr_done, "fr"), (f_xk, f_xk_done, "fk"))[k]
                dve.wait_ge(made[reader], due(dve, v))
                dve.wait_ge(f_diff, due(dve, v + 1))
                dve.scalar_tensor_tensor(out=dst[:, :], in0=fd[:, :], scalar=mu[:, k:k + 1], in1=fx[:, 0:SEQ],
                                         op0=ALU.mult, op1=ALU.add).then_inc(done, 1)

            def open_gate(v):
                if not active(v):
                    return
                dve.wait_ge(taken["fr"], due(dve, v + 1))
                dve.tensor_scalar(gate1[:, :], gate[:, :], 0.5, 0.5, ALU.mult, ALU.add).then_inc(gate_done, 1)

            def finish(v):
                if not active(v):
                    return
                dve.wait_ge(gate_done, due(dve, v + 1))
                dve.wait_ge(made["fv"], due(dve, v + 1))
                dve.tensor_tensor(gated[:, :], shared[:, :], gate1[:, :], ALU.mult).then_inc(taken["fv"], 1)
                dve.wait_ge(taken["fv"], due(dve, v + 1))
                dve.tensor_tensor(x_at(v + BATCH), gated[:, :], x_mid[:, :], ALU.add).then_inc(x_ready, 1)

            def body(u):
                for s in range(SLOTS):
                    for i in range(STEPS):
                        row_max(u, s, i)
                        for step, name, dv, k in ROUNDS[s]:
                            if step == i and name == "onat":
                                divide(u + dv, k)
                        if s == 0 and i in (4, 8):
                            rotate_cos(u + 1, 0 if i == 4 else 1)
                        if s == 0 and i == 11:
                            add_attn(u - 2)
                        if s == 1 and i == 0 and active(u - 2):
                            dve.wait_ge(taken["oproj"], due(dve, (u - 2) + 1))
                            stats(u - 2, 1, x_mid)
                        if s == 1 and i == 10:
                            shift_diff(u - 2)
                        if s == 1 and i == 11:
                            mix(u - 2, 1)
                        if s == 2 and i == 1:
                            mix(u - 2, 0)
                        if s == 2 and i == 8:
                            open_gate(u - 2)
                        if s == 2 and i == 10:
                            finish(u - 2)
                        if s == 3 and i == 2:
                            first_stats(u + 2)

            run(dve, body)

        @block.gpsimd
        def _(pool):
            pool.memset(ident[:, :], 0.0).then_inc(zeroed, 1)
            pool.memset(ident_b[:, :], 0.0).then_inc(zeroed, 1)
            pool.memset(causal[:, :], 0.0).then_inc(zeroed, 1)
            pool.memset(v_aug[:, :, :, :], 1.0).then_inc(setup, 1)
            pool.wait_ge(zeroed, 3)
            pool.affine_select(out=ident[:, :], in_=ident[:, :], compare_op=ALU.not_equal, fill=1.0, base=0,
                               pattern=[[-1, P]], channel_multiplier=1).then_inc(setup, 1)
            pool.affine_select(out=ident_b[:, :], in_=ident_b[:, :], compare_op=ALU.not_equal, fill=1.0, base=0,
                               pattern=[[-1, P]], channel_multiplier=1).then_inc(setup, 1)
            pool.affine_select(out=causal[:, :].rearrange("p (h k) -> p h k", h=GH),
                               in_=causal[:, :].rearrange("p (h k) -> p h k", h=GH), compare_op=ALU.is_ge,
                               fill=MASKED, base=0, pattern=[[0, GH], [-1, P]], channel_multiplier=1)\
                .then_inc(setup, 1)
            pool.wait_ge(const_in, 64)
            pool.sem_inc(setup, 1)
            pool.wait_ge(setup, SETUP)

            def copy(out, in_):
                return pool.tensor_copy(out, in_)

            def split_max(v, g):
                if not active(v):
                    return
                src, at = nmax[g % 2], v * 16 + 4 * g
                w, g0 = (v, g - 1) if g else (v - 1, 3)
                if active(w):
                    pool.wait_ge(made["max_t"], due(pool, w * 4 + (g0 + 1)))
                pool.wait_ge(p1_max, due(pool, v * (GROUPS * P1_UNITS) + P1_UNITS * (g + 1)))
                copy(nmax_p[:, :, :, :, 0], src[:, :, :, :]).then_inc(max_p, 1)
                pool.wait_ge(max_p, due(pool, at + 1))
                pool.tensor_tensor(nmax_r[:, :, :, :], src[:, :, :, :], nmax_p[:, :, :, :, 0], ALU.subtract).then_inc(max_p, 1)
                pool.wait_ge(max_p, due(pool, at + 2))
                copy(nmax_p[:, :, :, :, 1], nmax_r[:, :, :, :]).then_inc(max_p, 1)
                pool.wait_ge(max_p, due(pool, at + 3))
                pool.tensor_tensor(nmax_p[:, :, :, :, 2], nmax_r[:, :, :, :], nmax_p[:, :, :, :, 1], ALU.subtract)\
                    .then_inc(max_p, 1)

            def mask(v, g, kt):
                if not active(v):
                    return
                pool.wait_ge(exp_done, due(pool, v * (GROUPS * P2_UNITS) + (P2_UNITS * g + P2_UP_TO[kt])))
                blk = probs[g % 2][:, :, P_OFF[kt]:P_OFF[kt] + P]
                pool.affine_select(out=blk, in_=blk, compare_op=ALU.is_ge, fill=0.0, base=0,
                                   pattern=[[0, GH], [1, P]], channel_multiplier=-1).then_inc(mask_done, 1)

            def place_v(v, g):
                if not active(v):
                    return
                pool.wait_ge(taken["vproj"], due(pool, v + 1))
                pool.wait_ge(pv_full, due(pool, (v - 1) * 4 + (g + 1)))
                copy(v_aug[:, :, GH * g:GH * (g + 1), 0:DH], v_nat[:, :, GH * g:GH * (g + 1), :]).then_inc(v_copied, 1)

            def inv_std(v, which):
                if not active(v):
                    return
                pool.wait_ge(ln_done[which], due(pool, v * TILES))
                pool.wait_ge(ln_mv[which], due(pool, v + 1))
                pool.tensor_tensor(ve[which][:, :], mv[which][:, :, 1], eps_t[:, :], ALU.add).then_inc(ln_ve[which], 1)
                pool.wait_ge(ln_ve[which], due(pool, v + 1))
                pool.tensor_tensor(rstd[which][:, :], ve[which][:, :], mhalf[:, :], ALU.pow).then_inc(ln_rstd[which], 1)
                pool.tensor_tensor(nmean[which][:, :], zero_t[:, :], mv[which][:, :, 0], ALU.subtract).then_inc(ln_nmean[which], 1)
                pool.wait_ge(ln_rstd[which], due(pool, v + 1))
                pool.wait_ge(ln_nmean[which], due(pool, v + 1))
                pool.tensor_tensor(nbias[which][:, :], nmean[which][:, :], rstd[which][:, :], ALU.mult).then_inc(ln_bias[which], 1)

            def rotate(v, step):
                if not active(v):
                    return
                if step == 1:
                    pool.wait_ge(part2, due(pool, v))
                    pool.wait_ge(swap_in, due(pool, (v + 1) * 32))
                    pool.tensor_tensor(qk_rest[:, :], qk_sw[:, :], rope_table(v, 1), ALU.mult).then_inc(rope_s, 1)
                else:
                    pool.wait_ge(rope_c, due(pool, (v + 1) * 2))
                    pool.wait_ge(rope_s, due(pool, v + 1))
                    pool.tensor_tensor(qk_rot[:, :], qk_rot[:, :], qk_rest[:, :], ALU.add).then_inc(rope_done, 1)

            def rest(v, k):
                if not active(v):
                    return
                p = parts[:, k, :, :].rearrange("p a n -> p (a n)")
                if k == 0:
                    pool.wait_ge(rope_done, due(pool, v + 1))
                    pool.wait_ge(part0, due(pool, (v + 1) * 2))
                    pool.tensor_tensor(qk_rest[:, :], qk_rot[:, :], p, ALU.subtract).then_inc(rest0, 1)
                else:
                    pool.wait_ge(rest0, due(pool, v + 1))
                    pool.wait_ge(part1, due(pool, (v + 1) * 2))
                    pool.tensor_tensor(parts[:, 2, :, :].rearrange("p a n -> p (a n)"), qk_rest[:, :], p,
                                       ALU.subtract).then_inc(part2, 1)

            def square(v):
                if not active(v):
                    return
                pool.wait_ge(made["fv"], due(pool, v))
                pool.wait_ge(taken["fk"], due(pool, v + 1))
                pool.tensor_tensor(k_sq[:, :], k_relu[:, :], k_relu[:, :], ALU.mult).then_inc(sq_done, 1)

            def body(u):
                for s in range(SLOTS):
                    for i in range(STEPS):
                        if i == 0:
                            split_max(*max_group(u, s))
                        if i == 1:
                            place_v(u, s)
                        if i in MASK_AT:
                            mask(*pass2_group(u, s), MASK_AT[i])
                        if s == 1:
                            if i == 1:
                                inv_std(u - 2, 1)
                            if i == 2:
                                rotate(u + 1, 1)
                            if i == 4:
                                rotate(u + 1, 2)
                        if s == 2:
                            if i == 1:
                                rest(u + 1, 0)
                            if i == 2:
                                square(u - 2)
                            if i == 8:
                                rest(u + 1, 1)
                        if s == 3:
                            if i == 5:
                                inv_std(u + 2, 0)

            run(pool, body)


def kernel(**inputs):
    import numpy as np
    import concourse.bacc as bacc
    from concourse.bass_utils import run_bass_kernel_spmd

    a = {k: np.asarray(v) for k, v in inputs.items()}

    def cols(*mats):
        return np.ascontiguousarray(np.concatenate(mats, axis=1))

    def per_head(w):
        return w.reshape(DM, DM).T

    d_of = np.array([0, 2, 4, 6, 1, 3, 5, 7])
    order = np.array([(2 * pair + par) * DH + d for d in d_of for par in range(2) for pair in range(HEADS // 2)])
    w = cols(per_head(a["L0_attn_a_WQ"])[:, order], per_head(a["L0_attn_a_WK"])[:, order], per_head(a["L0_attn_a_WV"]),
             a["L0_attn_a_WO"].transpose(0, 2, 1).reshape(DM, DM),
             a["L0_attn_b_W_q"].T[:, order], a["L0_attn_b_W_k"].T[:, order], a["L0_attn_b_W_v"].T, a["L0_attn_b_W_o"].T)
    wf = cols(a["L0_ffn_W_r"].T, a["L0_ffn_W_k"].T, a["L0_ffn_W_v"].T)
    mu = np.ascontiguousarray(np.stack([a["L0_ffn_mu_r"], a["L0_ffn_mu_k"]], axis=1))

    inv_freq = (1.0 / 10000.0 ** (np.arange(0, DH, 2, dtype=np.float32) / np.float32(DH))).astype(np.float32)
    angle = (np.arange(SEQ, dtype=np.float32)[:, None] * inv_freq[None, :]).astype(np.float32)
    d = d_of[np.arange(P) // HEADS]
    cos = np.cos(angle.astype(np.float64)).T[d // 2]
    sin = np.sin(angle.astype(np.float64)).T[d // 2] * np.where(d % 2 == 0, -1.0, 1.0)[:, None]
    tables = []
    for c, s, scale in ((np.ones_like(cos), np.zeros_like(sin), DH ** -0.5), (cos, sin, DM ** -0.5)):
        tables += [c * scale, c, s * scale, s]
    rope = np.concatenate(tables, axis=1).astype(np.float32)

    arrays = {"x": np.ascontiguousarray(a["L0_attn_a_x"]), "w": w, "wf": wf, "mu": mu, "rope": rope}
    nc = bacc.Bacc("TRN2", target_bir_lowering=False, num_devices=1)
    args = [nc.dram_tensor(f"in_{n}", arr.shape, mybir.dt.from_np(arr.dtype), kind="ExternalInput").ap()
            for n, arr in arrays.items()]
    out = nc.dram_tensor("out", (BATCH, SEQ, DM), F32, kind="ExternalOutput").ap()
    build(nc, *args, out)
    r = run_bass_kernel_spmd(nc, [{f"in_{n}": arr for n, arr in arrays.items()}], core_ids=[0])
    return r.results[0]["out"]
```

```python
from contextlib import ExitStack

import concourse.bass as bass
from concourse import mybir

F32 = mybir.dt.float32
BF16 = mybir.dt.bfloat16
ALU = mybir.AluOpType
ACT = mybir.ActivationFunctionType
AX = mybir.AxisListType

P = 128
BATCH, SEQ, DM = 8, 512, 128
HEADS, DH = 16, 8
LAYERS = 2
UNITS = LAYERS * BATCH
TILES = SEQ // P
GROUPS, GH = 4, 4
SLOTS = GROUPS
PARTS = 3
Q_TERMS = [0, 0, 0, 1, 1, 2]
K_TERMS = [0, 1, 2, 0, 1, 0]
TERM_RUNS = [(0, 0, 3, 0, 0), (0, 3, 2, 1, 0), (0, 5, 1, 2, 0), (1, 0, 3, 0, 1), (1, 3, 2, 0, 1), (1, 5, 1, 0, 0)]
TERM_ROWS = DH * len(Q_TERMS)
AUG_ROWS = TERM_ROWS + PARTS
HALF = 64
OW = 32
EPS = 1e-5
MASKED = -3.0e38
TWO_ONES = 1.0 + 0x3F80 / 2.0 ** 23

P1_UNITS = 12
P2_UNITS = 12
RING = 3
P1_LIST = [(0, [0, 2]), (0, [1, 3]), (1, [0, 2]), (1, [1, 3])] + [(2, [j]) for j in range(4)] + [(3, [j]) for j in range(4)]
P2_LIST = [(0, [j]) for j in range(4)] + [(1, [j]) for j in range(4)] + [(2, [0, 2]), (2, [1, 3]), (3, [0, 2]), (3, [1, 3])]
P2_UP_TO = [4, 8, 10, 12]
P_OFF = [0, 512, 896, 1152]
P_LEN = 1280

STEPS = P1_UNITS
PV_AT = {2: 0, 5: 1, 8: 2, 10: 3}
MASK_AT = {3: 0, 7: 1, 9: 2, 11: 3}
ROUNDS = [
    [(1, "xn_t", 1, 0), (2, "attn_t", -2, 0), (4, "max_t", -1, 3), (5, "oproj", -2, 0), (8, "qproj", 1, 0),
     (10, "kproj", 1, 0)],
    [(3, "fx_t", -2, 0), (5, "max_t", 0, 0), (8, "fk", -2, 0), (10, "fr", -2, 0)],
    [(4, "max_t", 0, 1), (7, "fv", -2, 0)],
    [(1, "onat", -1, 0), (3, "max_t", 0, 2), (5, "onat", -1, 1), (7, "onat", -1, 2), (9, "onat", -1, 3),
     (11, "vproj", 1, 0)],
]
PER_UNIT = {"attn_t": 1, "max_t": 4, "oproj": 1, "xn_t": 1, "qproj": 1, "kproj": 1, "fx_t": 1, "fk": 1,
            "fr": 1, "onat": 4, "fv": 1, "vproj": 1}
FIRST_BODY, LOOP_FROM, LOOP_TO, LAST_BODY = -2, 3, UNITS - 2, UNITS + 1


def active(v):
    return not isinstance(v, int) or 0 <= v < UNITS


def turned(v):
    return not isinstance(v, int) or v > 0


def layer_of(v):
    return v // BATCH if isinstance(v, int) else (v >> 3).with_bounds(min_val=0, max_val=LAYERS - 1)


def max_group(u, s):
    return (u, s - 1) if s >= 1 else (u - 1, 3)


def pass2_group(u, s):
    return (u, s - 2) if s >= 2 else (u - 1, s + 2)


def pv_group(u, s):
    return (u, 0) if s == 3 else (u - 1, s + 1)


def build(nc, x_d, w_d, wf_d, mu_d, rope_d, out_d):
    with ExitStack() as ctx:
        def sb(name, shape, dt=F32):
            return ctx.enter_context(nc.sbuf_tensor(name, shape, dt))

        def ps(name, shape):
            return ctx.enter_context(nc.psum_tensor(name, shape, F32))

        def sem(name):
            return ctx.enter_context(nc.semaphore(name))

        x_sb = sb("x_sb", [P, UNITS * SEQ])
        w_all = sb("w_all", [P, LAYERS * 4 * DM])
        w_qkv = sb("w_qkv", [P, 3 * DM])
        w_o = sb("w_o", [P, DM])
        w_ffn = sb("w_ffn", [P, 3 * DM])
        mu = sb("mu", [P, 2])
        rope = sb("rope", [P, LAYERS * 2 * 2 * SEQ])
        ident = sb("ident", [P, P])
        ident_b = sb("ident_b", [P, P], BF16)
        causal = sb("causal", [P, GH * P], BF16)
        eps_t = sb("eps_t", [P, TILES])
        mhalf = sb("mhalf", [P, TILES])
        zero_t = sb("zero_t", [P, TILES])
        bn = [sb(f"bn{i}", [P, TILES, 6]) for i in range(2)]
        mv = [sb(f"mv{i}", [P, TILES, 2]) for i in range(2)]
        ve = [sb(f"ve{i}", [P, TILES]) for i in range(2)]
        rstd = [sb(f"rstd{i}", [P, TILES]) for i in range(2)]
        nmean = [sb(f"nmean{i}", [P, TILES]) for i in range(2)]
        nbias = [sb(f"nbias{i}", [P, TILES]) for i in range(2)]
        xn = [sb(f"xn{i}", [P, SEQ]) for i in range(2)]
        xn_t = sb("xn_t", [P, SEQ])
        qk = sb("qk", [P, 2 * SEQ])
        qk_sw = sb("qk_sw", [P, 2 * SEQ])
        qk_rot = sb("qk_rot", [P, 2 * SEQ])
        qk_rest = sb("qk_rest", [P, 2 * SEQ])
        parts = sb("parts", [P, PARTS, 2, SEQ], BF16)
        aug = sb("aug", [P, 2, HEADS // 2, SEQ], BF16)
        v_nat = sb("v_nat", [P, TILES, HEADS, DH])
        v_aug = sb("v_aug", [P, TILES, HEADS, OW])
        nmax = [sb(f"nmax{i}", [P, TILES, 2, 2]) for i in range(2)]
        nmax_r = sb("nmax_r", [P, TILES, 2, 2])
        nmax_p = sb("nmax_p", [P, TILES, 2, 2, PARTS], BF16)
        nmax_t = sb("nmax_t", [2 * PARTS * 2, SEQ], BF16)
        probs = [sb(f"probs{i}", [P, GH, P_LEN]) for i in range(2)]
        o_t = sb("o_t", [P, GROUPS, SEQ])
        rsum = sb("rsum", [P, TILES, HEADS])
        attn = sb("attn", [P, TILES, HEADS, DH])
        attn_t = sb("attn_t", [P, SEQ])
        x_mid = sb("x_mid", [P, SEQ])
        fx = sb("fx", [P, 1 + SEQ])
        fd = sb("fd", [P, SEQ])
        f_xk = sb("f_xk", [P, SEQ])
        f_xr = sb("f_xr", [P, SEQ])
        k_relu = sb("k_relu", [P, SEQ])
        k_sq = sb("k_sq", [P, SEQ])
        gate = sb("gate", [P, SEQ])
        gate1 = sb("gate1", [P, SEQ])
        gated = sb("gated", [P, SEQ])

        terms_d = nc.dram_tensor("terms", (2, len(Q_TERMS), P, SEQ), BF16).ap()

        p1 = ps("p1", [P, RING, 512])
        p2 = ps("p2", [P, RING, 512])
        pv = ps("pv", [P, 512])
        shared = ps("shared", [P, 512])
        shared_b = shared[:, :].bitcast(BF16)

        x_in = [sem(f"x_in{i}") for i in range(3)]
        w_all_in, const_in, rope_in = sem("w_all_in"), sem("const_in"), sem("rope_in")
        setup = sem("setup")
        zeroed = sem("zeroed")
        x_ready = sem("x_ready")
        w_in, wo_in, swap_in = sem("w_in"), sem("wo_in"), sem("swap_in")
        aug_in = [sem(f"aug_in{g}") for g in range(GROUPS)]
        terms_out = sem("terms_out")
        max_in = [sem(f"max_in{g}") for g in range(GROUPS)]
        made = {n: sem(f"made_{n}") for n in PER_UNIT}
        taken = {n: sem(f"taken_{n}") for n in PER_UNIT}
        ln_stat = [sem(f"ln_stat{i}") for i in range(2)]
        ln_mv = [sem(f"ln_mv{i}") for i in range(2)]
        ln_ve = [sem(f"ln_ve{i}") for i in range(2)]
        ln_rstd = [sem(f"ln_rstd{i}") for i in range(2)]
        ln_nmean = [sem(f"ln_nmean{i}") for i in range(2)]
        ln_bias = [sem(f"ln_bias{i}") for i in range(2)]
        ln_done = [sem(f"ln_done{i}") for i in range(2)]
        rope_c, rope_s, rope_done = sem("rope_c"), sem("rope_s"), sem("rope_done")
        part0, rest0, part1, part2 = sem("part0"), sem("rest0"), sem("part1"), sem("part2")
        v_copied = sem("v_copied")
        p1_full, p1_max = sem("p1_full"), sem("p1_max")
        max_p = sem("max_p")
        p2_full, exp_done, mask_done = sem("p2_full"), sem("exp_done"), sem("mask_done")
        pv_full, o_out = sem("pv_full"), sem("o_out")
        rsum_done = sem("rsum_done")
        f_diff, f_xk_done, f_xr_done, sq_done = sem("f_diff"), sem("f_xk_done"), sem("f_xr_done"), sem("sq_done")
        gate_done, gated_done = sem("gate_done"), sem("gated_done")
        out_done = sem("out_done")
        SETUP = 13

        block = ctx.enter_context(nc.Block())

        def due(eng, count):
            if isinstance(count, int):
                return max(count, 0)
            value = eng.to_reg(count)
            eng.wait_ge(setup, SETUP)
            return value

        def x_at(v):
            if isinstance(v, int):
                return x_sb[:, (v % UNITS) * SEQ:(v % UNITS + 1) * SEQ]
            return x_sb[:, bass.ds((v % UNITS) * SEQ, SEQ)]

        def rope_table(v, k, side=None):
            first, n = (0, 2 * SEQ) if side is None else (side * SEQ, SEQ)
            return rope[:, bass.ds(layer_of(v) * (4 * SEQ) + (k * 2 * SEQ + first), n)]

        def bank_before(u, s, step):
            order = [(ss, st, n, du, k) for ss in range(SLOTS) for st, n, du, k in ROUNDS[ss]]
            at = [(ss, st) for ss, st, *_ in order].index((s, step))
            for back in range(1, 3 * len(order)):
                i = at - back
                body = i // len(order)
                _, _, n, du, k = order[i % len(order)]
                v = u + (body + du)
                if isinstance(v, int) and v < 0 and u + body < FIRST_BODY:
                    return None
                if active(v):
                    return taken[n], v * PER_UNIT[n] + (k + 1)
            return None

        def run(eng, body):
            for u in range(FIRST_BODY, LOOP_FROM):
                body(u)
            with eng.Fori(LOOP_FROM, LOOP_TO) as u:
                body(u)
            for u in range(LOOP_TO, LAST_BODY + 1):
                body(u)

        @block.sync
        def _(sp):
            xr = x_d.rearrange("b (t p) d -> b p t d", p=P)

            def load_x(b, s):
                sp.dma_start(x_sb[:, b * SEQ:(b + 1) * SEQ].rearrange("p (t d) -> p t d", d=DM), xr[b]).then_inc(s, 16)

            load_x(0, x_in[0])
            sp.dma_start(w_all[:, :], w_d).then_inc(w_all_in, 16)
            sp.dma_start(w_ffn[:, :], wf_d).then_inc(const_in, 16)
            sp.dma_start(mu[:, :], mu_d).then_inc(const_in, 16)
            load_x(1, x_in[1])
            sp.wait_ge(w_all_in, 16)
            sp.wait_ge(setup, SETUP)

            def load_w(v):
                if not active(v):
                    return
                sp.wait_ge(made["vproj"], due(sp, v))
                layer = layer_of(v)
                sp.dma_start(w_qkv[:, :], w_all[:, bass.ds(layer * (4 * DM), 3 * DM)]).then_inc(w_in, 16)

            def load_wo(v):
                if not active(v):
                    return
                sp.wait_ge(made["oproj"], due(sp, v))
                layer = layer_of(v)
                sp.dma_start(w_o[:, :], w_all[:, bass.ds(layer * (4 * DM) + 3 * DM, DM)]).then_inc(wo_in, 16)

            def swap(v):
                if not active(v) or not turned(v):
                    return
                sp.wait_ge(taken["qproj"], due(sp, v + 1))
                sp.wait_ge(taken["kproj"], due(sp, v + 1))
                sp.wait_ge(rope_s, due(sp, v - 1))
                for k in range(2):
                    a, b = slice(k * HALF, (k + 1) * HALF), slice((1 - k) * HALF, (2 - k) * HALF)
                    sp.dma_start(qk_sw[a, :], qk[b, :]).then_inc(swap_in, 16)

            def send_terms(v):
                if not active(v):
                    return
                sp.wait_ge(part0, due(sp, (v + 1) * 2))
                sp.wait_ge(part1, due(sp, (v + 1) * 2))
                sp.wait_ge(part2, due(sp, (v + 1) * 2))
                for g in range(GROUPS):
                    sp.wait_ge(aug_in[g], due(sp, v * 32))
                for side, t0, n, part, step in TERM_RUNS:
                    src = parts[:, part, side, :].unsqueeze(1).broadcast_to([P, n, SEQ]) if step == 0 \
                        else parts[:, part:part + n, side, :]
                    sp.dma_start(terms_d[side, t0:t0 + n].rearrange("t p n -> p t n"), src).then_inc(terms_out, 16)

            def fetch_terms(v, g):
                if not active(v):
                    return
                sp.wait_ge(terms_out, due(sp, (v + 1) * (16 * len(TERM_RUNS))))
                sp.wait_ge(p2_full, due(sp, (v - 1) * (P2_UNITS * GROUPS) + P2_UNITS * (g + 1)))
                src = terms_d.rearrange("s t (d par pair) n -> par (t d) s pair n", par=2, d=DH)
                for par in range(2):
                    sp.dma_start(aug[HALF * par:HALF * par + TERM_ROWS, :, 2 * g:2 * g + 2, :],
                                 src[par][:, :, 2 * g:2 * g + 2, :]).then_inc(aug_in[g], 16)

            def put_max(v, g):
                if not active(v):
                    return
                sp.wait_ge(taken["max_t"], due(sp, v * 4 + (g + 1)))
                for par in range(2):
                    row = HALF * par + TERM_ROWS
                    for jj in range(2):
                        src = nmax_t[6 * par + 3 * jj:6 * par + 3 * jj + PARTS, :]
                        sp.dma_start(aug[row:row + PARTS, 0, 2 * g + jj, :], src).then_inc(max_in[g], 16)

            def body(u):
                if isinstance(u, int) and u == -1:
                    sp.dma_start(rope[:, 4 * SEQ:8 * SEQ], rope_d).then_inc(rope_in, 16)
                    for b in range(2, BATCH):
                        load_x(b, x_in[2])
                fetch_terms(u, 1)
                put_max(u - 1, 3)
                swap(u + 1)
                fetch_terms(u, 2)
                put_max(u, 0)
                load_wo(u - 1)
                fetch_terms(u, 3)
                put_max(u, 1)
                send_terms(u + 1)
                put_max(u, 2)
                fetch_terms(u + 1, 0)
                load_w(u + 2)

            run(sp, body)
            orr = out_d.rearrange("b (t p) d -> b p t d", p=P)
            for b in range(BATCH):
                sp.wait_ge(x_ready, 2 * BATCH + b + 1)
                sp.dma_start(orr[b], x_sb[:, b * SEQ:(b + 1) * SEQ].rearrange("p (t d) -> p t d", d=DM)).then_inc(out_done, 16)
            sp.wait_ge(out_done, 16 * BATCH)

        @block.tensor
        def _(pe):
            pe.wait_ge(setup, SETUP)
            pe.wait_ge(const_in, 32)

            def pass1(u, g, i):
                if not active(u):
                    return
                if i == 0:
                    pe.wait_ge(aug_in[g], due(pe, (u + 1) * 32))
                n = GROUPS * P1_UNITS
                pe.wait_ge(p1_max, due(pe, u * n + (P1_UNITS * g + i - RING + 1)))
                bank = i % RING
                qt, heads = P1_LIST[i]
                length = (qt + 1) * P
                out = p1[:, bank, 0:len(heads) * length].rearrange("p (h k) -> p h k", h=len(heads))
                pe.matmul(out[:, :, qt * P:length], ident_b[:, :],
                          causal[:, 0:len(heads) * P].rearrange("p (h k) -> p h k", h=len(heads)),
                          start=True, stop=False, skip_group_check=True)
                for n_, j in enumerate(heads):
                    row, pair = HALF * (j % 2), 2 * g + j // 2
                    last = pe.matmul(out[:, n_, :], aug[row:row + TERM_ROWS, 0, pair, qt * P:(qt + 1) * P],
                                     aug[row:row + TERM_ROWS, 1, pair, 0:length],
                                     start=False, stop=True, skip_group_check=True)
                last.then_inc(p1_full, 1)

            def pass2(v, g, i):
                if not active(v):
                    return
                if i == 0:
                    pe.wait_ge(max_in[g], due(pe, (v + 1) * (16 * 4)))
                n = GROUPS * P2_UNITS
                pe.wait_ge(exp_done, due(pe, v * n + (P2_UNITS * g + i - RING + 1)))
                kt, heads = P2_LIST[i]
                width = SEQ - kt * P
                for m, j in enumerate(heads):
                    row, pair = HALF * (j % 2), 2 * g + j // 2
                    last = pe.matmul(p2[:, i % RING, m * width:(m + 1) * width],
                                     aug[row:row + AUG_ROWS, 1, pair, kt * P:(kt + 1) * P],
                                     aug[row:row + AUG_ROWS, 0, pair, kt * P:SEQ], start=True, stop=True)
                last.then_inc(p2_full, 1)

            def times_v(v, g, kt):
                if not active(v):
                    return
                if kt == 0:
                    if isinstance(v, int):
                        pe.wait_ge(o_out, due(pe, v * 4 + g))
                pe.wait_ge(mask_done, due(pe, v * 16 + (4 * g + kt + 1)))
                for j in range(GH):
                    last = pe.matmul(pv[OW * j:OW * (j + 1), kt * P:SEQ], v_aug[:, kt, GH * g + j, :],
                                     probs[g % 2][:, j, P_OFF[kt]:P_OFF[kt] + SEQ - kt * P],
                                     start=(kt == 0), stop=(kt == TILES - 1), tile_position=(0, OW * j))
                if kt == TILES - 1:
                    last.then_inc(pv_full, 1)

            def tile_t(i):
                return slice(i * P, (i + 1) * P)

            def shared_round(u, s, step, name, dv, k):
                v = u + dv
                if not active(v):
                    return
                before = bank_before(u, s, step)
                if name == "xn_t":
                    pe.wait_ge(ln_done[0], due(pe, (v + 1) * TILES))
                    if before:
                        pe.wait_ge(before[0], due(pe, before[1]))
                    for t in range(TILES):
                        last = pe.transpose(shared[:, tile_t(t)], xn[0][:, tile_t(t)], ident[:, :])
                elif name in ("qproj", "kproj"):
                    if name == "qproj":
                        pe.wait_ge(taken["xn_t"], due(pe, v + 1))
                        pe.wait_ge(w_in, due(pe, (v + 1) * 16))
                    w = 0 if name == "qproj" else 1
                    if before:
                        pe.wait_ge(before[0], due(pe, before[1]))
                    last = pe.matmul(shared[:, :], w_qkv[:, tile_t(w)], xn_t[:, :], start=True, stop=True)
                elif name == "vproj":
                    if before:
                        pe.wait_ge(before[0], due(pe, before[1]))
                    for t in range(TILES):
                        last = pe.matmul(shared[:, tile_t(t)], xn_t[:, tile_t(t)], w_qkv[:, tile_t(2)], start=True, stop=True)
                elif name == "max_t":
                    pe.wait_ge(max_p, due(pe, v * 16 + (4 * k + 4)))
                    if before:
                        pe.wait_ge(before[0], due(pe, before[1]))
                    for t in range(TILES):
                        last = pe.transpose(shared_b[0:4 * PARTS, tile_t(t)],
                                            nmax_p[:, t, :, :, :].rearrange("p a b k -> p (a b k)"), ident_b[:, :])
                elif name == "onat":
                    if k == 0:
                        pe.wait_ge(o_out, due(pe, v * 4 + 4))
                    if before:
                        pe.wait_ge(before[0], due(pe, before[1]))
                    for g in range(GROUPS):
                        last = pe.transpose(shared[:, tile_t(g)], o_t[:, g, tile_t(k)], ident[:, :])
                elif name == "attn_t":
                    if before:
                        pe.wait_ge(before[0], due(pe, before[1]))
                    for t in range(TILES):
                        last = pe.transpose(shared[:, tile_t(t)], attn[:, t, :, :].rearrange("p h d -> p (h d)"), ident[:, :])
                elif name == "oproj":
                    pe.wait_ge(taken["attn_t"], due(pe, v + 1))
                    pe.wait_ge(wo_in, due(pe, (v + 1) * 16))
                    if before:
                        pe.wait_ge(before[0], due(pe, before[1]))
                    for t in range(TILES):
                        last = pe.matmul(shared[:, tile_t(t)], attn_t[:, tile_t(t)], w_o[:, :], start=True, stop=True)
                elif name == "fx_t":
                    pe.wait_ge(ln_done[1], due(pe, (v + 1) * TILES))
                    if before:
                        pe.wait_ge(before[0], due(pe, before[1]))
                    for t in range(TILES):
                        last = pe.transpose(shared[:, tile_t(t)], xn[1][:, tile_t(t)], ident[:, :])
                elif name == "fk":
                    pe.wait_ge(f_xk_done, due(pe, v + 1))
                    if before:
                        pe.wait_ge(before[0], due(pe, before[1]))
                    last = pe.matmul(shared[:, :], w_ffn[:, tile_t(1)], f_xk[:, :], start=True, stop=True)
                elif name == "fr":
                    pe.wait_ge(f_xr_done, due(pe, v + 1))
                    if before:
                        pe.wait_ge(before[0], due(pe, before[1]))
                    for t in range(TILES):
                        last = pe.matmul(shared[:, tile_t(t)], f_xr[:, tile_t(t)], w_ffn[:, tile_t(0)], start=True, stop=True)
                elif name == "fv":
                    pe.wait_ge(sq_done, due(pe, v + 1))
                    if before:
                        pe.wait_ge(before[0], due(pe, before[1]))
                    for t in range(TILES):
                        last = pe.matmul(shared[:, tile_t(t)], k_sq[:, tile_t(t)], w_ffn[:, tile_t(2)], start=True, stop=True)
                last.then_inc(made[name], 1)

            def body(u):
                for s in range(SLOTS):
                    for i in range(STEPS):
                        pass1(u, s, i)
                        pass2(*pass2_group(u, s), i)
                        if i in PV_AT:
                            times_v(*pv_group(u, s), PV_AT[i])
                        for step, name, dv, k in ROUNDS[s]:
                            if step == i:
                                shared_round(u, s, step, name, dv, k)

            run(pe, body)

        @block.scalar
        def _(act):
            act.wait_ge(setup, SETUP)

            def exps(v, g, i):
                if not active(v):
                    return
                if i == 0:
                    act.wait_ge(pv_full, due(act, v * 4 + (g - 1)))
                act.wait_ge(p2_full, due(act, v * (GROUPS * P2_UNITS) + (P2_UNITS * g + i + 1)))
                kt, heads = P2_LIST[i]
                width = SEQ - kt * P
                src = p2[:, i % RING, 0:len(heads) * width].rearrange("p (h q) -> p h q", h=len(heads))
                dst = probs[g % 2][:, heads[0]:heads[-1] + 1:2, P_OFF[kt]:P_OFF[kt] + width]
                act.activation(dst, src, ACT.Exp).then_inc(exp_done, 1)

            def out_copy(v, g):
                if not active(v):
                    return
                act.wait_ge(made["onat"], due(act, v * 4))
                act.wait_ge(pv_full, due(act, v * 4 + (g + 1)))
                act.copy(o_t[:, g, :], pv[:, :]).then_inc(o_out, 1)

            def take(v, name, k):
                if not active(v) or name in ("onat", "oproj", "fv"):
                    return
                if name == "xn_t":
                    act.wait_ge(made["vproj"], due(act, v))
                    act.wait_ge(made["xn_t"], due(act, v + 1))
                    act.copy(xn_t[:, :], shared[:, :]).then_inc(taken[name], 1)
                elif name in ("qproj", "kproj"):
                    side = 0 if name == "qproj" else 1
                    act.wait_ge(swap_in, due(act, (v - 1) * 32))
                    act.wait_ge(rope_c, due(act, v * 2))
                    act.wait_ge(made[name], due(act, v + 1))
                    act.copy(qk[:, side * SEQ:(side + 1) * SEQ], shared[:, :]).then_inc(taken[name], 1)
                elif name == "vproj":
                    act.wait_ge(v_copied, due(act, v * 4))
                    act.wait_ge(made[name], due(act, v + 1))
                    act.copy(v_nat[:, :, :, :].rearrange("p t h d -> p (t h d)"), shared[:, :]).then_inc(taken[name], 1)
                elif name == "max_t":
                    w, k0 = (v, k - 1) if k else (v - 1, 3)
                    if active(w):
                        act.wait_ge(max_in[k0], due(act, (w + 1) * (16 * 4)))
                    act.wait_ge(made[name], due(act, v * 4 + (k + 1)))
                    act.copy(nmax_t[:, :], shared_b[0:4 * PARTS, 0:SEQ]).then_inc(taken[name], 1)
                elif name == "attn_t":
                    act.wait_ge(made["oproj"], due(act, v))
                    act.wait_ge(made[name], due(act, v + 1))
                    act.copy(attn_t[:, :], shared[:, :]).then_inc(taken[name], 1)
                elif name == "fx_t":
                    act.wait_ge(f_xk_done, due(act, v))
                    act.wait_ge(f_xr_done, due(act, v))
                    act.wait_ge(made[name], due(act, v + 1))
                    act.copy(fx[:, 1:1 + SEQ], shared[:, :]).then_inc(taken[name], 1)
                elif name == "fk":
                    act.wait_ge(sq_done, due(act, v))
                    act.wait_ge(made[name], due(act, v + 1))
                    act.activation(k_relu[:, :], shared[:, :], ACT.Relu).then_inc(taken[name], 1)
                elif name == "fr":
                    act.wait_ge(gate_done, due(act, v))
                    act.wait_ge(made[name], due(act, v + 1))
                    act.activation(gate[:, :], shared[:, :], ACT.Tanh, scale=0.5).then_inc(taken[name], 1)

            def normalise(v, which, x, t):
                if not active(v):
                    return
                if t == 0:
                    act.wait_ge(ln_rstd[which], due(act, v + 1))
                    act.wait_ge(ln_bias[which], due(act, v + 1))
                    act.wait_ge(made["xn_t" if which == 0 else "fx_t"], due(act, v))
                act.activation(xn[which][:, t * P:(t + 1) * P], x[:, t * P:(t + 1) * P], ACT.Identity,
                               scale=rstd[which][:, t:t + 1], bias=nbias[which][:, t:t + 1]).then_inc(ln_done[which], 1)

            def cast_part(v, k, side):
                if not active(v):
                    return
                half = slice(side * SEQ, (side + 1) * SEQ)
                if k == 0:
                    act.wait_ge(terms_out, due(act, v * (16 * len(TERM_RUNS))))
                    if turned(v):
                        act.wait_ge(rope_done, due(act, v))
                    else:
                        act.wait_ge(rope_c, 2)
                    act.copy(parts[:, 0, side, :], qk_rot[:, half]).then_inc(part0, 1)
                else:
                    act.wait_ge(rest0, due(act, v * 2 + (side + 1)))
                    act.copy(parts[:, 1, side, :], qk_rest[:, half]).then_inc(part1, 1)

            def body(u):
                for s in range(SLOTS):
                    for i in range(STEPS):
                        if i == 11:
                            out_copy(*pv_group(u, s))
                        exps(*pass2_group(u, s), i)
                        for step, name, dv, k in ROUNDS[s]:
                            if step == i:
                                take(u + dv, name, k)
                        if (s, i) in ((0, 10), (0, 11), (1, 0), (1, 1)):
                            normalise(u - 2, 1, x_mid, (i + 2) % STEPS)
                        if (s, i) in ((1, 11), (2, 1)):
                            cast_part(u + 1, 0, s - 1)
                        if s == 2 and i in (5, 7):
                            cast_part(u + 1, 1, i // 2 - 2)
                        if s == 3 and 4 <= i < 4 + TILES and active(u + 2):
                            normalise(u + 2, 0, x_at(u + 2), i - 4)

            run(act, body)

        @block.vector
        def _(dve):
            dve.memset(fx[:, 0:1], 0.0).then_inc(setup, 1)
            dve.memset(eps_t[:, :], EPS).then_inc(setup, 1)
            dve.memset(mhalf[:, :], -0.5).then_inc(setup, 1)
            dve.memset(zero_t[:, :], 0.0).then_inc(setup, 1)
            dve.memset(rope[:, 0:SEQ], DH ** -0.5).then_inc(setup, 1)
            dve.memset(rope[:, SEQ:2 * SEQ], 1.0).then_inc(setup, 1)
            for par in range(2):
                ones = slice(HALF * par + HALF // 2, HALF * (par + 1))
                dve.memset(aug[ones, 1, :, :].rearrange("p a n -> p (a n)").bitcast(F32), TWO_ONES).then_inc(setup, 1)
            dve.wait_ge(x_in[0], 16)
            dve.sem_inc(x_ready, BATCH)
            dve.wait_ge(setup, SETUP)

            def row_max(u, g, i):
                if not active(u):
                    return
                if i == 0:
                    w, g0 = (u, g - 2) if g >= 2 else (u - 1, g + 2)
                    if active(w):
                        dve.wait_ge(max_p, due(dve, w * 16 + (4 * g0 + 3)))
                dve.wait_ge(p1_full, due(dve, u * (GROUPS * P1_UNITS) + (P1_UNITS * g + i + 1)))
                qt, heads = P1_LIST[i]
                length = (qt + 1) * P
                src = p1[:, i % RING, 0:len(heads) * length].rearrange("p (h k) -> p h k", h=len(heads))
                jj, par = heads[0] // 2, heads[0] % 2
                if len(heads) == 2:
                    dst = nmax[g % 2][:, qt, par, :]
                else:
                    dst = nmax[g % 2][:, qt, par, jj:jj + 1]
                dve.tensor_reduce(dst, src, AX.X, ALU.max, negate=True).then_inc(p1_max, 1)

            def stats(v, which, x, t):
                if not active(v):
                    return
                if t == 0:
                    dve.wait_ge(ln_bias[which], due(dve, v))
                dve.bn_stats(bn[which][:, t, :], x[:, t * P:(t + 1) * P]).then_inc(ln_stat[which], 1)

            def mean_var(v, which):
                if not active(v):
                    return
                dve.wait_ge(ln_stat[which], due(dve, (v + 1) * TILES))
                for t in range(TILES):
                    last = dve.bn_aggr(mv[which][:, t, :], bn[which][:, t, :])
                last.then_inc(ln_mv[which], 1)

            def first_stats(v, t):
                if not active(v):
                    return
                if t == 0:
                    if isinstance(v, int) and v < 3:
                        dve.wait_ge(x_in[v], 16 if v < 2 else 16 * (BATCH - 2))
                    dve.wait_ge(x_ready, due(dve, v + 1))
                stats(v, 0, x_at(v), t)

            def divide(v, k):
                if not active(v):
                    return
                if k == 0:
                    dve.wait_ge(made["attn_t"], due(dve, v))
                dve.wait_ge(made["onat"], due(dve, v * 4 + (k + 1)))
                o = shared[:, :].rearrange("p (h c) -> p h c", c=OW)
                dve.reciprocal(rsum[:, k, :], o[:, :, DH]).then_inc(rsum_done, 1)
                dve.wait_ge(rsum_done, due(dve, v * 4 + (k + 1)))
                dve.tensor_tensor(attn[:, k, :, :], o[:, :, 0:DH],
                                  rsum[:, k, :].unsqueeze(2).broadcast_to([P, HEADS, DH]), ALU.mult)\
                    .then_inc(taken["onat"], 1)

            def add_attn(v):
                if not active(v):
                    return
                dve.wait_ge(made["oproj"], due(dve, v + 1))
                dve.wait_ge(x_ready, due(dve, v + BATCH))
                dve.tensor_tensor(x_mid[:, :], shared[:, :], x_at(v), ALU.add).then_inc(taken["oproj"], 1)

            def rotate_cos(v, side):
                if not active(v):
                    return
                if isinstance(v, int) and v == 2:
                    dve.wait_ge(rope_in, 16)
                half = slice(side * SEQ, (side + 1) * SEQ)
                dve.wait_ge(part0, due(dve, v * 2))
                dve.wait_ge(rest0, due(dve, v * 2))
                dve.wait_ge(taken["kproj" if side else "qproj"], due(dve, v + 1))
                dve.tensor_tensor(qk_rot[:, half], qk[:, half], rope_table(v, 0, side), ALU.mult).then_inc(rope_c, 1)

            def shift_diff(v):
                if not active(v):
                    return
                dve.wait_ge(f_xk_done, due(dve, v))
                dve.wait_ge(f_xr_done, due(dve, v))
                dve.wait_ge(taken["fx_t"], due(dve, v + 1))
                dve.tensor_tensor(fd[:, :], fx[:, 1:1 + SEQ], fx[:, 0:SEQ], ALU.subtract).then_inc(f_diff, 1)

            def mix(v, k):
                if not active(v):
                    return
                dst, done, reader = ((f_xr, f_xr_done, "fr"), (f_xk, f_xk_done, "fk"))[k]
                dve.wait_ge(made[reader], due(dve, v))
                dve.wait_ge(f_diff, due(dve, v + 1))
                dve.scalar_tensor_tensor(out=dst[:, :], in0=fd[:, :], scalar=mu[:, k:k + 1], in1=fx[:, 0:SEQ],
                                         op0=ALU.mult, op1=ALU.add).then_inc(done, 1)

            def open_gate(v):
                if not active(v):
                    return
                dve.wait_ge(taken["fr"], due(dve, v + 1))
                dve.tensor_scalar(gate1[:, :], gate[:, :], 0.5, 0.5, ALU.mult, ALU.add).then_inc(gate_done, 1)

            def use_gate(v):
                if not active(v):
                    return
                dve.wait_ge(x_ready, due(dve, BATCH + v))
                dve.wait_ge(gate_done, due(dve, v + 1))
                dve.wait_ge(made["fv"], due(dve, v + 1))
                dve.tensor_tensor(gated[:, :], shared[:, :], gate1[:, :], ALU.mult).then_inc(taken["fv"], 1)

            def body(u):
                for s in range(SLOTS):
                    for i in range(STEPS):
                        row_max(u, s, i)
                        for step, name, dv, k in ROUNDS[s]:
                            if step == i and name == "onat":
                                divide(u + dv, k)
                        if s == 1 and i in (0, 1):
                            rotate_cos(u + 1, i)
                        if s == 0 and i == 5:
                            add_attn(u - 2)
                        if s == 0 and i in (6, 7) and active(u - 2):
                            if i == 6:
                                dve.wait_ge(taken["oproj"], due(dve, (u - 2) + 1))
                            stats(u - 2, 1, x_mid, 2 * i - 12)
                            stats(u - 2, 1, x_mid, 2 * i - 11)
                        if s == 0 and i == 7:
                            mean_var(u - 2, 1)
                        if s == 1 and i == 4:
                            shift_diff(u - 2)
                        if s == 1 and i == 5:
                            mix(u - 2, 1)
                        if s == 1 and i == 7:
                            mix(u - 2, 0)
                        if s == 1 and i == 11:
                            open_gate(u - 2)
                        if s == 2 and i == 8:
                            use_gate(u - 2)
                        if s == 2 and 2 <= i < 2 + TILES:
                            first_stats(u + 2, i - 2)
                        if s == 2 and i == 6:
                            mean_var(u + 2, 0)

            run(dve, body)

        @block.gpsimd
        def _(pool):
            pool.memset(ident[:, :], 0.0).then_inc(zeroed, 1)
            pool.memset(ident_b[:, :], 0.0).then_inc(zeroed, 1)
            pool.memset(causal[:, :], 0.0).then_inc(zeroed, 1)
            pool.memset(v_aug[:, :, :, :], 1.0).then_inc(setup, 1)
            pool.memset(rope[:, 2 * SEQ:4 * SEQ], 0.0).then_inc(setup, 1)
            pool.wait_ge(zeroed, 3)
            pool.affine_select(out=ident[:, :], in_=ident[:, :], compare_op=ALU.not_equal, fill=1.0, base=0,
                               pattern=[[-1, P]], channel_multiplier=1).then_inc(setup, 1)
            pool.affine_select(out=ident_b[:, :], in_=ident_b[:, :], compare_op=ALU.not_equal, fill=1.0, base=0,
                               pattern=[[-1, P]], channel_multiplier=1).then_inc(setup, 1)
            pool.affine_select(out=causal[:, :].rearrange("p (h k) -> p h k", h=GH),
                               in_=causal[:, :].rearrange("p (h k) -> p h k", h=GH), compare_op=ALU.is_ge,
                               fill=MASKED, base=0, pattern=[[0, GH], [-1, P]], channel_multiplier=1)\
                .then_inc(setup, 1)
            pool.wait_ge(setup, SETUP)

            def copy(out, in_):
                return pool.tensor_copy(out, in_)

            def split_max(v, g):
                if not active(v):
                    return
                src, at = nmax[g % 2], v * 16 + 4 * g
                w, g0 = (v, g - 1) if g else (v - 1, 3)
                if active(w):
                    pool.wait_ge(made["max_t"], due(pool, w * 4 + (g0 + 1)))
                pool.wait_ge(p1_max, due(pool, v * (GROUPS * P1_UNITS) + P1_UNITS * (g + 1)))
                copy(nmax_p[:, :, :, :, 0], src[:, :, :, :]).then_inc(max_p, 1)
                pool.wait_ge(max_p, due(pool, at + 1))
                pool.tensor_tensor(nmax_r[:, :, :, :], src[:, :, :, :], nmax_p[:, :, :, :, 0], ALU.subtract).then_inc(max_p, 1)
                pool.wait_ge(max_p, due(pool, at + 2))
                copy(nmax_p[:, :, :, :, 1], nmax_r[:, :, :, :]).then_inc(max_p, 1)
                pool.wait_ge(max_p, due(pool, at + 3))
                pool.tensor_tensor(nmax_p[:, :, :, :, 2], nmax_r[:, :, :, :], nmax_p[:, :, :, :, 1], ALU.subtract)\
                    .then_inc(max_p, 1)

            def mask(v, g, kt):
                if not active(v):
                    return
                pool.wait_ge(exp_done, due(pool, v * (GROUPS * P2_UNITS) + (P2_UNITS * g + P2_UP_TO[kt])))
                blk = probs[g % 2][:, :, P_OFF[kt]:P_OFF[kt] + P]
                pool.affine_select(out=blk, in_=blk, compare_op=ALU.is_ge, fill=0.0, base=0,
                                   pattern=[[0, GH], [1, P]], channel_multiplier=-1).then_inc(mask_done, 1)

            def place_v(v, g):
                if not active(v):
                    return
                pool.wait_ge(taken["vproj"], due(pool, v + 1))
                pool.wait_ge(pv_full, due(pool, (v - 1) * 4 + (g + 1)))
                copy(v_aug[:, :, GH * g:GH * (g + 1), 0:DH], v_nat[:, :, GH * g:GH * (g + 1), :]).then_inc(v_copied, 1)

            def inv_std(v, which):
                if not active(v):
                    return
                pool.wait_ge(ln_done[which], due(pool, v * TILES))
                pool.wait_ge(ln_mv[which], due(pool, v + 1))
                pool.tensor_tensor(ve[which][:, :], mv[which][:, :, 1], eps_t[:, :], ALU.add).then_inc(ln_ve[which], 1)
                pool.wait_ge(ln_ve[which], due(pool, v + 1))
                pool.tensor_tensor(rstd[which][:, :], ve[which][:, :], mhalf[:, :], ALU.pow).then_inc(ln_rstd[which], 1)
                pool.tensor_tensor(nmean[which][:, :], zero_t[:, :], mv[which][:, :, 0], ALU.subtract).then_inc(ln_nmean[which], 1)
                pool.wait_ge(ln_rstd[which], due(pool, v + 1))
                pool.wait_ge(ln_nmean[which], due(pool, v + 1))
                pool.tensor_tensor(nbias[which][:, :], nmean[which][:, :], rstd[which][:, :], ALU.mult).then_inc(ln_bias[which], 1)

            def rotate(v, step):
                if not active(v) or not turned(v):
                    return
                if isinstance(v, int) and v == 2:
                    pool.wait_ge(rope_in, 16)
                if step == 1:
                    pool.wait_ge(part2, due(pool, v * 2))
                    pool.wait_ge(swap_in, due(pool, v * 32))
                    pool.tensor_tensor(qk_rest[:, :], qk_sw[:, :], rope_table(v, 1), ALU.mult).then_inc(rope_s, 1)
                else:
                    pool.wait_ge(rope_c, due(pool, (v + 1) * 2))
                    pool.wait_ge(rope_s, due(pool, v))
                    pool.tensor_tensor(qk_rot[:, :], qk_rot[:, :], qk_rest[:, :], ALU.add).then_inc(rope_done, 1)

            def rest(v, k, side):
                if not active(v):
                    return
                half = slice(side * SEQ, (side + 1) * SEQ)
                pool.wait_ge((part0, part1)[k], due(pool, v * 2 + (side + 1)))
                if k == 0:
                    pool.tensor_tensor(qk_rest[:, half], qk_rot[:, half], parts[:, 0, side, :], ALU.subtract).then_inc(rest0, 1)
                else:
                    pool.tensor_tensor(parts[:, 2, side, :], qk_rest[:, half], parts[:, 1, side, :],
                                       ALU.subtract).then_inc(part2, 1)

            def add_ffn(v):
                if not active(v):
                    return
                pool.wait_ge(taken["fv"], due(pool, v + 1))
                pool.tensor_tensor(x_at(v + BATCH), gated[:, :], x_mid[:, :], ALU.add).then_inc(x_ready, 1)

            def square(v):
                if not active(v):
                    return
                pool.wait_ge(made["fv"], due(pool, v))
                pool.wait_ge(taken["fk"], due(pool, v + 1))
                pool.tensor_tensor(k_sq[:, :], k_relu[:, :], k_relu[:, :], ALU.mult).then_inc(sq_done, 1)

            def body(u):
                for s in range(SLOTS):
                    for i in range(STEPS):
                        if i == 0:
                            split_max(*max_group(u, s))
                        if i == 1:
                            place_v(u, s)
                        if i in MASK_AT:
                            mask(*pass2_group(u, s), MASK_AT[i])
                        if s == 0:
                            if i == 8:
                                inv_std(u - 2, 1)
                        if s == 1:
                            if i == 3:
                                rotate(u + 1, 1)
                            if i == 6:
                                rotate(u + 1, 2)
                        if s == 2:
                            if i == 1:
                                square(u - 2)
                            if i in (1, 3):
                                rest(u + 1, 0, i // 2)
                            if i in (6, 8):
                                rest(u + 1, 1, i // 2 - 3)
                        if s == 3:
                            if i == 2:
                                add_ffn(u - 2)
                            if i == 1:
                                inv_std(u + 2, 0)

            run(pool, body)


def kernel(**inputs):
    import numpy as np
    import concourse.bacc as bacc
    from concourse.bass_utils import run_bass_kernel_spmd

    a = {k: np.asarray(v) for k, v in inputs.items()}

    def cols(*mats):
        return np.ascontiguousarray(np.concatenate(mats, axis=1))

    def per_head(w):
        return w.reshape(DM, DM).T

    d_of = np.array([0, 2, 4, 6, 1, 3, 5, 7])
    order = np.array([(2 * pair + par) * DH + d for d in d_of for par in range(2) for pair in range(HEADS // 2)])
    w = cols(per_head(a["L0_attn_a_WQ"])[:, order], per_head(a["L0_attn_a_WK"])[:, order], per_head(a["L0_attn_a_WV"]),
             a["L0_attn_a_WO"].transpose(0, 2, 1).reshape(DM, DM),
             a["L0_attn_b_W_q"].T[:, order], a["L0_attn_b_W_k"].T[:, order], a["L0_attn_b_W_v"].T, a["L0_attn_b_W_o"].T)
    wf = cols(a["L0_ffn_W_r"].T, a["L0_ffn_W_k"].T, a["L0_ffn_W_v"].T)
    mu = np.ascontiguousarray(np.stack([a["L0_ffn_mu_r"], a["L0_ffn_mu_k"]], axis=1))

    inv_freq = (1.0 / 10000.0 ** (np.arange(0, DH, 2, dtype=np.float32) / np.float32(DH))).astype(np.float32)
    angle = (np.arange(SEQ, dtype=np.float32)[:, None] * inv_freq[None, :]).astype(np.float32)
    d = d_of[np.arange(P) // HEADS]
    cos = np.cos(angle.astype(np.float64)).T[d // 2]
    sin = np.sin(angle.astype(np.float64)).T[d // 2] * np.where(d % 2 == 0, -1.0, 1.0)[:, None]
    scale = DM ** -0.5
    rope = np.concatenate([cos * scale, cos, sin * scale, sin], axis=1).astype(np.float32)

    arrays = {"x": np.ascontiguousarray(a["L0_attn_a_x"]), "w": w, "wf": wf, "mu": mu, "rope": rope}
    nc = bacc.Bacc("TRN2", target_bir_lowering=False, num_devices=1)
    args = [nc.dram_tensor(f"in_{n}", arr.shape, mybir.dt.from_np(arr.dtype), kind="ExternalInput").ap()
            for n, arr in arrays.items()]
    out = nc.dram_tensor("out", (BATCH, SEQ, DM), F32, kind="ExternalOutput").ap()
    build(nc, *args, out)
    r = run_bass_kernel_spmd(nc, [{f"in_{n}": arr for n, arr in arrays.items()}], core_ids=[0])
    return r.results[0]["out"]
```
